# Optimizing a Trainium2 kernel written in Bass

```python
import numpy as np
import jax
import jax.numpy as jnp

def _softmax(x, axis=-1):
    return jax.nn.softmax(x, axis=axis)

def _gelu(x):
    return jax.nn.gelu(x, approximate=True)

def _silu(x):
    return jax.nn.silu(x)

def _sigmoid(x):
    return jax.nn.sigmoid(x)

def _layernorm(x, axis=-1, eps=1e-05):
    m = jnp.mean(x, axis=axis, keepdims=True)
    v = jnp.var(x, axis=axis, keepdims=True)
    return (x - m) / jnp.sqrt(v + eps)

def _scatter_add(tgt, idx, src, axis=0):
    return tgt.at[idx].add(src)

def _segment_sum(src, seg, n):
    return jax.ops.segment_sum(src, seg, n)
kernel_name = 'mk_xattn_ffn_d1_seqx_r4_7cec41'

def setup_inputs(seed: int=0):
    np.random.seed(seed)
    _w = jnp.asarray

    def _rec_inputs():
        import jax
        import jax.numpy as jnp
        _rk = jax.random.key(seed)
        x = -1.394e-06 + 0.9999 * jax.random.normal(jax.random.fold_in(_rk, 1), (32, 256, 256), jnp.float32)
        _lenS = 256 - jax.random.randint(jax.random.fold_in(_rk, 7), (32,), 0, max(1, 256 // 4) + 1, jnp.int32)
        _lenS2 = 77 - jax.random.randint(jax.random.fold_in(_rk, 8), (32,), 0, max(1, 77 // 4) + 1, jnp.int32)
        _ctx_1024P = jax.random.normal(jax.random.fold_in(_rk, 11), (32, 16, 256), jnp.float32)
        _ctx_1024c = jax.random.dirichlet(jax.random.fold_in(_rk, 511), 0.3 * jnp.ones((16,), jnp.float32), (32, 77))
        _ctx_1024t = jnp.einsum('bsk,bkd->bsd', _ctx_1024c, _ctx_1024P)
        _ctx_1024t = _ctx_1024t * jax.lax.rsqrt(jnp.mean(jnp.square(_ctx_1024t)) + 1e-12) * 0.953939
        ctx_1024 = -0.000392918 + 0.999932 * (_ctx_1024t + 0.3 * jax.random.normal(jax.random.fold_in(_rk, 611), (32, 77, 256), jnp.float32))
        _validS = jnp.arange(256)[None, :] < _lenS[:, None]
        _validS2 = jnp.arange(77)[None, :] < _lenS2[:, None]
        _causal = jnp.tril(jnp.ones((256, 256), dtype=bool))
        mask_BxS2_bk0 = jnp.logical_not(jnp.broadcast_to(_validS2[:, :], (32, 77)))
        return (x, ctx_1024, mask_BxS2_bk0)
    x, ctx_1024, mask_BxS2_bk0 = _rec_inputs()

    def _L0_xattn_setup():
        import jax, jax.numpy as jnp
        import numpy as np
        DIM = 256
        DIM_LATENT = 256
        DIM_HEAD = 64
        INNER = max(DIM, DIM_LATENT)
        HEADS = INNER // DIM_HEAD
        SCALE = DIM_HEAD ** (-0.5)
        LN_EPS = 1e-05
        RMS_EPS = 1e-08

        def layernorm(x, g, b):
            mu = jnp.mean(x, axis=-1, keepdims=True)
            var = jnp.mean(jnp.square(x - mu), axis=-1, keepdims=True)
            return (x - mu) * jax.lax.rsqrt(var + LN_EPS) * g + b

        def rmsnorm(x, gamma):
            n = jnp.linalg.norm(x, axis=-1, keepdims=True) * x.shape[-1] ** (-0.5)
            return x / jnp.maximum(n, RMS_EPS) * gamma
        key = jax.random.key(seed)
        ks = jax.random.split(key, 8)
        b, n, nl = (8, 512, 128)
        x = jax.random.normal(ks[0], (b, n, DIM), dtype=jnp.float32)
        latents = jax.random.normal(ks[1], (b, nl, DIM_LATENT), dtype=jnp.float32)
        mask = jax.random.randint(ks[2], (b, n), 0, 2).astype(bool)
        init = lambda k, shape, fan_in: jax.random.normal(k, shape, jnp.float32) * fan_in ** (-0.5)
        return {'x': x, 'latents': latents, 'mask': mask, 'ln_x_g': jnp.ones((DIM,), jnp.float32), 'ln_x_b': jnp.zeros((DIM,), jnp.float32), 'ln_l_g': jnp.ones((DIM_LATENT,), jnp.float32), 'ln_l_b': jnp.zeros((DIM_LATENT,), jnp.float32), 'q_gamma': jnp.ones((DIM_HEAD,), jnp.float32), 'k_gamma': jnp.ones((DIM_HEAD,), jnp.float32), 'W_q': init(ks[3], (DIM_LATENT, INNER), DIM_LATENT), 'W_kv': init(ks[4], (DIM, 2 * INNER), DIM), 'W_out': init(ks[5], (INNER, DIM_LATENT), INNER), 'b_out': jnp.zeros((DIM_LATENT,), jnp.float32)}
    _L0_xattn_all = _L0_xattn_setup()
    _L0_xattn_in = {k: v for k, v in _L0_xattn_all.items() if k in ('ln_x_g', 'ln_x_b', 'ln_l_g', 'ln_l_b', 'q_gamma', 'k_gamma', 'W_q', 'W_kv', 'W_out', 'b_out')}
    del _L0_xattn_all

    def _L0_ffn_setup():
        import jax, jax.numpy as jnp
        import numpy as np
        B, S, H = (2, 256, 256)
        E, I, SI = (8, 128, 512)
        TOP_K, N_GROUP, TOPK_GROUP = (2, 2, 1)
        ROUTED_SCALE = 2.5

        def _route(x2d, gate_weight, gate_bias):
            T = x2d.shape[0]
            logits = x2d @ gate_weight.T
            scores = jax.nn.sigmoid(logits)
            sfc = scores + gate_bias[None, :]
            g = sfc.reshape(T, N_GROUP, E // N_GROUP)
            group_scores = jax.lax.top_k(g, 2)[0].sum(-1)
            _, gidx = jax.lax.top_k(group_scores, TOPK_GROUP)
            gmask = jnp.zeros((T, N_GROUP), sfc.dtype).at[jnp.arange(T)[:, None], gidx].set(1.0)
            smask = jnp.repeat(gmask, E // N_GROUP, axis=1)
            masked = jnp.where(smask > 0, sfc, 0.0)
            _, topk_idx = jax.lax.top_k(masked, TOP_K)
            topk_w = jnp.take_along_axis(scores, topk_idx, axis=1)
            topk_w = topk_w / (topk_w.sum(-1, keepdims=True) + 1e-20)
            topk_w = topk_w * ROUTED_SCALE
            return (topk_idx, topk_w)
        key = jax.random.key(seed)
        ks = jax.random.split(key, 7)

        def w(k, shape, sc=0.02):
            return jax.random.normal(k, shape, jnp.float32) * sc
        return {'hidden_states': jax.random.normal(ks[0], (B, S, H), jnp.float32), 'gate_weight': w(ks[1], (E, H)), 'gate_bias': w(ks[2], (E,), 0.01), 'up_weights': w(ks[3], (E, I, H)), 'down_weights': w(ks[4], (E, H, I)), 'shared_up_weight': w(ks[5], (SI, H)), 'shared_down_weight': w(ks[6], (H, SI))}
    _L0_ffn_all = _L0_ffn_setup()
    _L0_ffn_in = {k: v for k, v in _L0_ffn_all.items() if k in ('gate_weight', 'gate_bias', 'up_weights', 'down_weights', 'shared_up_weight', 'shared_down_weight')}
    del _L0_ffn_all
    return {'x': x, 'ctx_1024': ctx_1024, 'mask_BxS2_bk0': mask_BxS2_bk0, 'L0_xattn_ln_x_g': _L0_xattn_in['ln_x_g'], 'L0_xattn_ln_x_b': _L0_xattn_in['ln_x_b'], 'L0_xattn_ln_l_g': _L0_xattn_in['ln_l_g'], 'L0_xattn_ln_l_b': _L0_xattn_in['ln_l_b'], 'L0_xattn_q_gamma': _L0_xattn_in['q_gamma'], 'L0_xattn_k_gamma': _L0_xattn_in['k_gamma'], 'L0_xattn_W_q': _L0_xattn_in['W_q'], 'L0_xattn_W_kv': _L0_xattn_in['W_kv'], 'L0_xattn_W_out': _L0_xattn_in['W_out'], 'L0_xattn_b_out': _L0_xattn_in['b_out'], 'L0_ffn_gate_weight': _L0_ffn_in['gate_weight'], 'L0_ffn_gate_bias': _L0_ffn_in['gate_bias'], 'L0_ffn_up_weights': _L0_ffn_in['up_weights'], 'L0_ffn_down_weights': _L0_ffn_in['down_weights'], 'L0_ffn_shared_up_weight': _L0_ffn_in['shared_up_weight'], 'L0_ffn_shared_down_weight': _L0_ffn_in['shared_down_weight']}

def reference(x, ctx_1024, mask_BxS2_bk0, L0_xattn_ln_x_g, L0_xattn_ln_x_b, L0_xattn_ln_l_g, L0_xattn_ln_l_b, L0_xattn_q_gamma, L0_xattn_k_gamma, L0_xattn_W_q, L0_xattn_W_kv, L0_xattn_W_out, L0_xattn_b_out, L0_ffn_gate_weight, L0_ffn_gate_bias, L0_ffn_up_weights, L0_ffn_down_weights, L0_ffn_shared_up_weight, L0_ffn_shared_down_weight):
    import jax
    import jax.numpy as jnp

    def _L0_xattn_ref(x, latents, mask, ln_x_g, ln_x_b, ln_l_g, ln_l_b, q_gamma, k_gamma, W_q, W_kv, W_out, b_out):
        import jax, jax.numpy as jnp
        import numpy as np
        DIM = 256
        DIM_LATENT = 256
        DIM_HEAD = 64
        INNER = max(DIM, DIM_LATENT)
        HEADS = INNER // DIM_HEAD
        SCALE = DIM_HEAD ** (-0.5)
        LN_EPS = 1e-05
        RMS_EPS = 1e-08

        def layernorm(x, g, b):
            mu = jnp.mean(x, axis=-1, keepdims=True)
            var = jnp.mean(jnp.square(x - mu), axis=-1, keepdims=True)
            return (x - mu) * jax.lax.rsqrt(var + LN_EPS) * g + b

        def rmsnorm(x, gamma):
            n = jnp.linalg.norm(x, axis=-1, keepdims=True) * x.shape[-1] ** (-0.5)
            return x / jnp.maximum(n, RMS_EPS) * gamma
        b, n, _ = x.shape
        nl = latents.shape[1]
        xn = layernorm(x, ln_x_g, ln_x_b)
        ln = layernorm(latents, ln_l_g, ln_l_b)
        q = ln @ W_q
        kv = jnp.concatenate([xn @ W_kv, ln @ W_kv], axis=1)
        k, v = (kv[..., :INNER], kv[..., INNER:])
        to_heads = lambda t: t.reshape(t.shape[0], t.shape[1], HEADS, DIM_HEAD).transpose(0, 2, 1, 3)
        q, k, v = (to_heads(q), to_heads(k), to_heads(v))
        qn = rmsnorm(q, q_gamma) * SCALE
        kn = rmsnorm(k, k_gamma)
        sim = jnp.einsum('bhid,bhjd->bhij', qn, kn)
        full_mask = jnp.pad(mask, ((0, 0), (0, nl)), constant_values=True)
        neg = -jnp.finfo(sim.dtype).max
        sim = jnp.where(full_mask[:, None, None, :], sim, neg)
        attn = jax.nn.softmax(sim.astype(jnp.float32), axis=-1).astype(sim.dtype)
        out = jnp.einsum('bhij,bhjd->bhid', attn, v)
        out = out.transpose(0, 2, 1, 3).reshape(b, nl, INNER)
        return out @ W_out + b_out

    def _L0_ffn_ref(hidden_states, gate_weight, gate_bias, up_weights, down_weights, shared_up_weight, shared_down_weight):
        import jax, jax.numpy as jnp
        import numpy as np
        B, S, H = (2, 256, 256)
        E, I, SI = (8, 128, 512)
        TOP_K, N_GROUP, TOPK_GROUP = (2, 2, 1)
        ROUTED_SCALE = 2.5

        def _route(x2d, gate_weight, gate_bias):
            T = x2d.shape[0]
            logits = x2d @ gate_weight.T
            scores = jax.nn.sigmoid(logits)
            sfc = scores + gate_bias[None, :]
            g = sfc.reshape(T, N_GROUP, E // N_GROUP)
            group_scores = jax.lax.top_k(g, 2)[0].sum(-1)
            _, gidx = jax.lax.top_k(group_scores, TOPK_GROUP)
            gmask = jnp.zeros((T, N_GROUP), sfc.dtype).at[jnp.arange(T)[:, None], gidx].set(1.0)
            smask = jnp.repeat(gmask, E // N_GROUP, axis=1)
            masked = jnp.where(smask > 0, sfc, 0.0)
            _, topk_idx = jax.lax.top_k(masked, TOP_K)
            topk_w = jnp.take_along_axis(scores, topk_idx, axis=1)
            topk_w = topk_w / (topk_w.sum(-1, keepdims=True) + 1e-20)
            topk_w = topk_w * ROUTED_SCALE
            return (topk_idx, topk_w)
        Bv, Sv, Hv = hidden_states.shape
        x = hidden_states.reshape(-1, Hv)
        T = x.shape[0]
        topk_idx, topk_w = _route(x, gate_weight, gate_bias)
        cw = jnp.zeros((T, E), x.dtype).at[jnp.arange(T)[:, None], topk_idx].add(topk_w)
        h = jnp.einsum('th,eih->tei', x, up_weights)
        r = jnp.maximum(h, 0.0)
        r2 = r * r
        routed = jnp.einsum('tei,ehi,te->th', r2, down_weights, cw)
        sh = jnp.maximum(x @ shared_up_weight.T, 0.0)
        shared = sh * sh @ shared_down_weight.T
        return (routed + shared).reshape(Bv, Sv, Hv)
    x = x + _L0_xattn_ref(ctx_1024, _layernorm(x, axis=-1), mask_BxS2_bk0, L0_xattn_ln_x_g, L0_xattn_ln_x_b, L0_xattn_ln_l_g, L0_xattn_ln_l_b, L0_xattn_q_gamma, L0_xattn_k_gamma, L0_xattn_W_q, L0_xattn_W_kv, L0_xattn_W_out, L0_xattn_b_out)
    x = x + _L0_ffn_ref(_layernorm(x, axis=-1), L0_ffn_gate_weight, L0_ffn_gate_bias, L0_ffn_up_weights, L0_ffn_down_weights, L0_ffn_shared_up_weight, L0_ffn_shared_down_weight)
    return x

_drawn_inputs = setup_inputs


def setup_inputs(seed=0):
    import zlib

    import numpy as np

    out = dict(_drawn_inputs(seed))
    spreads = {'L0_xattn_ln_x_g': (1.0, 0.6),
     'L0_xattn_ln_x_b': (0.0, 0.8),
     'L0_xattn_ln_l_g': (1.0, 0.2),
     'L0_xattn_ln_l_b': (0.0, 0.1),
     'L0_xattn_q_gamma': (1.0, 0.539),
     'L0_xattn_k_gamma': (1.0, 0.2),
     'L0_xattn_b_out': (0.0, 0.1)}
    factors = {'L0_ffn_gate_bias': 3.851}
    for name, (base, spread) in spreads.items():
        noise = np.random.default_rng([zlib.crc32(name.encode()), seed]).standard_normal(out[name].shape)
        drawn = base * np.exp(spread * noise) if base else spread * noise
        out[name] = jnp.asarray(drawn.astype(out[name].dtype))
    for name, factor in factors.items():
        out[name] = (out[name] * factor).astype(out[name].dtype)
    return out
```

```python
from contextlib import ExitStack

import concourse.bass as bass
from concourse import mybir

F32 = mybir.dt.float32
F32R = mybir.dt.float32r
U8 = mybir.dt.uint8
ALU = mybir.AluOpType
ACT = mybir.ActivationFunctionType
AX_X = mybir.AxisListType.X

LN_EPS = 1e-5
RMS_EPS = 1e-8
MASKED = 3.0e38
ROUTED_SCALE = 2.5
DMA = 16


def build(nc, x, ctx_in, mask, g_x, b_x, g_l, b_l, q_gamma, k_gamma, w_q, w_kv, w_out, b_out,
          gate_t, gate_bias, up_t, down_t, out):
    B, S, D = x.shape
    C = ctx_in.shape[1]
    P = 128
    DH = q_gamma.shape[0]
    H = D // DH
    T = S // P
    FT = D // P
    KEYS = S + C
    CH = 3
    KC = KEYS // CH
    KPAD = KEYS + KEYS % 2
    E = gate_t.shape[1]
    F = up_t.shape[1] // P
    FS = F - E
    PAIRS = F // 2
    SP_PAIRS = FS // 2
    U = T * H
    G = E // 4
    assert KC * CH == KEYS and KC <= P and D == 256 and S == 256 and 2 * DH == P and FS == 4
    ACC = 1 + 2 * E

    with ExitStack() as stack:
        def sb(name, shape, dt=F32):
            return stack.enter_context(nc.sbuf_tensor(name, shape, dt))

        def sem(name):
            return stack.enter_context(nc.semaphore(name))

        ident = sb("ident", [P, P])
        head_sel = sb("head_sel", [P, 2])
        lower = sb("lower", [P, E, E])
        minus_half = sb("minus_half", [P, 16])
        ln_g = sb("ln_g", [P, 2, FT])
        ln_b = sb("ln_b", [P, 2, FT])
        gam_q = sb("gam_q", [P, 1])
        gam_k = sb("gam_k", [P, 1])
        gam_qk = sb("gam_qk", [P, 1])
        bout_row = sb("bout_row", [P, D])
        gbias = sb("gbias", [P, E])
        w_stage = sb("w_stage", [P, FT, 4 * D])
        up_stage = sb("up_stage", [P, FT, F * P])
        down_stage = sb("down_stage", [P, F, D])
        gate_stage = sb("gate_stage", [P, FT, E])
        w_hi, w_lo = sb("w_hi", [P, FT, 4 * D], F32R), sb("w_lo", [P, FT, 4 * D], F32R)
        up_hi, up_lo = sb("up_hi", [P, FT, F * P], F32R), sb("up_lo", [P, FT, F * P], F32R)
        down_hi, down_lo = sb("down_hi", [P, F, D], F32R), sb("down_lo", [P, F, D], F32R)
        gate_hi, gate_lo = sb("gate_hi", [P, FT, E], F32R), sb("gate_lo", [P, FT, E], F32R)

        x_in = sb("x_in", [P, T, D])
        c_in = sb("c_in", [C, D])
        mask_in = sb("mask_in", [P, C], U8)
        mask_row = sb("mask_row", [P, KEYS])
        x_res = sb("x_res", [P, T, D])
        stats1 = sb("stats1", [P, T + 1, 6])
        mv1 = sb("mv1", [P, T + 1, 2])
        var1 = sb("var1", [P, T + 1])
        rstd1 = sb("rstd1", [P, T + 1])
        x_hat = sb("x_hat", [P, T, D])
        c_hat = sb("c_hat", [C, D])
        ln_t = sb("ln_t", [P, FT, KEYS])
        ln_hi, ln_lo = sb("ln_hi", [P, FT, KEYS], F32R), sb("ln_lo", [P, FT, KEYS], F32R)
        q_hi, q_lo = sb("q_hi", [P, FT, S], F32R), sb("q_lo", [P, FT, S], F32R)
        q_sq = sb("q_sq", [P, FT, S])
        q_norm = sb("q_norm", [P, U])
        q_scale = sb("q_scale", [P, U])
        k_sq = sb("k_sq", [KC, CH, D])
        k_sum = sb("k_sum", [KC, CH * H])
        k_norm = sb("k_norm", [KC, CH * H])
        k_scale = sb("k_scale", [KC, CH * H])
        k_rms = sb("k_rms", [KC, CH, D])
        v_sb = sb("v_sb", [KC, CH, D])
        k_hi, k_lo = sb("k_hi", [P, FT, KPAD], F32R), sb("k_lo", [P, FT, KPAD], F32R)

        masked = sb("masked", [P, U, KEYS])
        row_max = sb("row_max", [P, U])
        neg_max = sb("neg_max", [P, U])
        probs = sb("probs", [P, U, KEYS])
        row_sum = sb("row_sum", [P, U])
        row_inv = sb("row_inv", [P, U])
        PT_RING = 3
        probs_t = sb("probs_t", [KC, PT_RING, CH * P])
        attn = sb("attn", [P, U, DH])
        at_hi, at_lo = sb("at_hi", [P, FT, S], F32R), sb("at_lo", [P, FT, S], F32R)
        x1 = sb("x1", [P, T, D])
        stats2 = sb("stats2", [P, T, 6])
        mv2 = sb("mv2", [P, T, 2])
        var2 = sb("var2", [P, T])
        rstd2 = sb("rstd2", [P, T])
        x2_hat = sb("x2_hat", [P, T, D])
        x2_hi, x2_lo = sb("x2_hi", [P, FT, S], F32R), sb("x2_lo", [P, FT, S], F32R)

        exp_neg = sb("exp_neg", [P, T, E])
        sig_den = sb("sig_den", [P, T, E])
        score = sb("score", [P, T, E])
        biased = sb("biased", [P, T, E])
        pair_hi = sb("pair_hi", [P, T * G, 2])
        pair_lo = sb("pair_lo", [P, T * G, 2])
        top1 = sb("top1", [P, T * G])
        mid_a = sb("mid_a", [P, T * G])
        mid_b = sb("mid_b", [P, T * G])
        top2 = sb("top2", [P, T * G])
        group_sum = sb("group_sum", [P, T, G])
        group_sel = sb("group_sel", [P, T, G])
        in_group = sb("in_group", [P, T, E])
        above = sb("above", [P, T, E, E])
        tied = sb("tied", [P, T, E, E])
        tied_low = sb("tied_low", [P, T, E, E])
        beats = sb("beats", [P, T, E, E])
        rank = sb("rank", [P, T, E])
        picked = sb("picked", [P, T, E])
        pick_sum = sb("pick_sum", [P, T])
        pick_eps = sb("pick_eps", [P, T])
        pick_inv = sb("pick_inv", [P, T])
        route_w = sb("route_w", [P, T, E])
        relu_sb = sb("relu_sb", [P, 2, 2 * S])
        relu2 = sb("relu2", [P, 2, 2 * S])
        HID_RING = 3
        hid_hi = sb("hid_hi", [P, HID_RING, 2 * S], F32R)
        hid_lo = sb("hid_lo", [P, HID_RING, 2 * S], F32R)
        acc = sb("acc", [P, T, D])
        carrier = sb("carrier", [P, 1])

        attn_ps = stack.enter_context(nc.psum_tensor("attn_ps", [P, 4, 512], F32))
        up_ps = stack.enter_context(nc.psum_tensor("up_ps", [P, 2, 512], F32))
        down_ps = stack.enter_context(nc.psum_tensor("down_ps", [P, 2, 512], F32))

        weights_in, up_in, down_in = sem("weights_in"), sem("up_in"), sem("down_in")
        vectors_in = sem("vectors_in")
        x_loaded, c_loaded, mask_loaded = sem("x_loaded"), sem("c_loaded"), sem("mask_loaded")
        stored = sem("stored")
        consts, zeroed = sem("consts"), sem("zeroed")
        w_hi_done, w_lo_done = sem("w_hi_done"), sem("w_lo_done")
        gamma_done, head_sel_done = sem("gamma_done"), sem("head_sel_done")
        lnt_ps, q_ps, kv_ps, qn_ps, kt_ps = sem("lnt_ps"), sem("q_ps"), sem("kv_ps"), sem("qn_ps"), sem("kt_ps")
        score_ps, pt_ps, pv_ps = sem("score_ps"), sem("pt_ps"), sem("pv_ps")
        at_ps, out_ps, x2t_ps, logit_ps = sem("at_ps"), sem("out_ps"), sem("x2t_ps"), sem("logit_ps")
        up_done, down_done = sem("up_done"), sem("down_done")
        ln_full_done = sem("ln_full_done")
        q_hi_done, q_sq_done = sem("q_hi_done"), sem("q_sq_done")
        k_sq_done, v_done, k_hi_done = sem("k_sq_done"), sem("v_done"), sem("k_hi_done")
        prob_done, pt_done = sem("prob_done"), sem("pt_done")
        at_hi_done, x2_hi_done, exp_neg_done = sem("at_hi_done"), sem("x2_hi_done"), sem("exp_neg_done")
        relu_done, relu2_done = sem("relu_done"), sem("relu2_done")
        ln1_step, var1_done, x_hat_done, mask_done = sem("ln1_step"), sem("var1_done"), sem("x_hat_done"), sem("mask_done")
        ln_hi_done, q_lo_done, q_norm_done = sem("ln_hi_done"), sem("q_lo_done"), sem("q_norm_done")
        k_sum_done, k_norm_done, k_rms_done, k_lo_done = sem("k_sum_done"), sem("k_norm_done"), sem("k_rms_done"), sem("k_lo_done")
        masked_done, neg_max_done = sem("masked_done"), sem("neg_max_done")
        row_inv_done, attn_done, at_lo_done, x1_done = sem("row_inv_done"), sem("attn_done"), sem("at_lo_done"), sem("x1_done")
        ln2_step, var2_done, x2_hat_done, x2_lo_done = sem("ln2_step"), sem("var2_done"), sem("x2_hat_done"), sem("x2_lo_done")
        router_step, hid_hi_done, acc_done = sem("router_step"), sem("hid_hi_done"), sem("acc_done")
        rstd1_done, ln_lo_done, x_res_done = sem("rstd1_done"), sem("ln_lo_done"), sem("x_res_done")
        q_scale_done, k_scale_done, rstd2_done, hid_lo_done = sem("q_scale_done"), sem("k_scale_done"), sem("rstd2_done"), sem("hid_lo_done")

        LN1_STEPS = 2 * (T + 1)
        LN2_STEPS = 2 * T
        ROUTER_STEPS = 23

        block = stack.enter_context(nc.Block())

        def steps(eng, step):
            step(0, False, True)
            step(1, True, True)
            with eng.Fori(2, B - 1) as b:
                step(b, True, True)
            step(B - 1, True, False)

        @block.sync
        def _(sp):
            def load(b, first):
                if not first:
                    sp.wait_ge(x_hat_done, b)
                    sp.wait_ge(x_res_done, b)
                    sp.wait_ge(mask_done, b)
                sp.dma_start(x_in[:], x[b].rearrange("(t p) d -> p t d", p=P)).then_inc(x_loaded, DMA)
                sp.dma_start(c_in[:], ctx_in[b]).then_inc(c_loaded, DMA)
                sp.dma_start(mask_in[:], mask[b].partition_broadcast(P)).then_inc(mask_loaded, DMA)

            def store(b):
                sp.wait_ge(acc_done, b * ACC + ACC)
                sp.dma_start(out[b].rearrange("(t p) d -> p t d", p=P), acc[:]).then_inc(stored, DMA)

            load(0, True)
            sp.dma_start(w_stage[:, :, 0:D], w_q.rearrange("(k p) n -> p k n", p=P)).then_inc(weights_in, DMA)
            sp.dma_start(w_stage[:, :, D:3 * D], w_kv.rearrange("(k p) n -> p k n", p=P)).then_inc(weights_in, DMA)
            sp.dma_start(w_stage[:, :, 3 * D:4 * D], w_out.rearrange("(k p) n -> p k n", p=P)).then_inc(weights_in, DMA)
            sp.dma_start(gate_stage[:], gate_t.rearrange("(k p) n -> p k n", p=P)).then_inc(weights_in, DMA)
            sp.dma_start(up_stage[:], up_t.rearrange("(k p) n -> p k n", p=P)).then_inc(up_in, DMA)
            sp.dma_start(down_stage[:], down_t.rearrange("(f p) n -> p f n", p=P)).then_inc(down_in, DMA)
            load(1, False)

            def step(b, experts, following):
                if following and not (isinstance(b, int) and b == 0):
                    load(b + 1, False)
                if experts:
                    store(b - 1)

            steps(sp, step)
            store(B - 1)
            sp.wait_ge(stored, B * DMA)

        @block.tensor
        def _(pe):
            def split_product(out_ap, stationary, moving, first, last):
                (s_hi, s_lo), (m_hi, m_lo) = stationary, moving
                nc.tensor.matmul(out_ap, s_hi, m_hi, start=first, stop=False)
                nc.tensor.matmul(out_ap, s_hi, m_lo, start=False, stop=False)
                return nc.tensor.matmul(out_ap, s_lo, m_hi, start=False, stop=last)

            def transpose_ln(b, first):
                pe.wait_ge(x_hat_done, b + 1)
                for ft in range(FT):
                    if not first:
                        pe.wait_ge(pt_done, b * U - (2 if ft == 0 else 1))
                    for t in range(T):
                        nc.tensor.transpose(attn_ps[:, 1 + ft, t * P:(t + 1) * P], x_hat[:, t, ft * P:(ft + 1) * P], ident[:])
                    nc.tensor.transpose(attn_ps[:, 1 + ft, S:KEYS], c_hat[:, ft * P:(ft + 1) * P],
                                        ident[0:C, 0:C]).then_inc(lnt_ps, 1)

            def project_q(b):
                pe.wait_ge(ln_hi_done, b + 1)
                pe.wait_ge(ln_lo_done, b + 1)
                for ft in range(FT):
                    for k in range(FT):
                        cols = slice(ft * P, (ft + 1) * P)
                        last = split_product(attn_ps[:, 0, ft * S:(ft + 1) * S],
                                             (w_hi[:, k, cols], w_lo[:, k, cols]),
                                             (ln_hi[:, k, 0:S], ln_lo[:, k, 0:S]), k == 0, k == FT - 1)
                last.then_inc(q_ps, 1)

            def project_kv(b, c):
                if c == 0:
                    pe.wait_ge(q_sq_done, b + 1)
                    pe.wait_ge(q_lo_done, b + 1)
                rows = slice(c * KC, (c + 1) * KC)
                for k in range(FT):
                    last = split_product(attn_ps[0:KC, c, :], (ln_hi[:, k, rows], ln_lo[:, k, rows]),
                                         (w_hi[:, k, D:3 * D], w_lo[:, k, D:3 * D]), k == 0, k == FT - 1)
                last.then_inc(kv_ps, 1)

            def sum_q_squares(b, first):
                pe.wait_ge(q_sq_done, b + 1)
                if first:
                    pe.wait_ge(head_sel_done, 1)
                if not first:
                    pe.wait_ge(x1_done, b)
                for t in range(T):
                    for ft in range(FT):
                        last = nc.tensor.matmul(attn_ps[:, 3, t * H + 2 * ft:t * H + 2 * ft + 2],
                                                q_sq[:, ft, t * P:(t + 1) * P], head_sel[:], start=True, stop=True)
                last.then_inc(qn_ps, 1)

            def transpose_k(b):
                pe.wait_ge(k_rms_done, b + 1)
                pe.wait_ge(v_done, b + 1)
                for ft in range(FT):
                    for c in range(CH):
                        last = nc.tensor.transpose(attn_ps[:, ft, c * KC:(c + 1) * KC],
                                                   k_rms[:, c, ft * P:(ft + 1) * P], ident[0:KC, 0:KC])
                    last.then_inc(kt_ps, 1)

            def scores(b, u):
                t, h = divmod(u, H)
                if u < 2:
                    pe.wait_ge(k_hi_done, b * FT + u + 1)
                    pe.wait_ge(k_lo_done, b * FT + u + 1)
                elif u >= 3:
                    pe.wait_ge(masked_done, b * U + u - 2)
                ft, rows = h // 2, slice((h % 2) * DH, (h % 2 + 1) * DH)
                cols = slice(t * P, (t + 1) * P)
                split_product(attn_ps[:, u % 3, 0:KPAD], (q_hi[rows, ft, cols], q_lo[rows, ft, cols]),
                              (k_hi[rows, ft, :], k_lo[rows, ft, :]), True, True).then_inc(score_ps, 1)

            def transpose_probs(b, u):
                pe.wait_ge(prob_done, b * U + u + 1)
                if u < 3:
                    pe.wait_ge(masked_done, b * U + 6 + u)
                else:
                    pe.wait_ge(pt_done, b * U + u - 2)
                for c in range(CH):
                    last = nc.tensor.transpose(attn_ps[0:KC, (u + 2) % 3, c * P:(c + 1) * P],
                                               probs[:, u, c * KC:(c + 1) * KC], ident[:])
                last.then_inc(pt_ps, 1)

            def probs_times_v(b, u, first):
                if u == 0:
                    pe.wait_ge(q_norm_done, b + 1)
                    if not first:
                        pe.wait_ge(exp_neg_done, b)
                pe.wait_ge(pt_done, b * U + u + 1)
                h = u % H
                for c in range(CH):
                    last = nc.tensor.matmul(attn_ps[:, 3, u * DH:(u + 1) * DH],
                                            probs_t[:, u % PT_RING, c * P:(c + 1) * P],
                                            v_sb[:, c, h * DH:(h + 1) * DH], start=(c == 0), stop=(c == CH - 1))
                last.then_inc(pv_ps, 1)

            def transpose_attn(b):
                pe.wait_ge(attn_done, b + 1)
                pe.wait_ge(pt_done, b * U + U)
                for t in range(T):
                    for ft in range(FT):
                        last = nc.tensor.transpose(attn_ps[:, 0, ft * S + t * P:ft * S + (t + 1) * P],
                                                   attn[:, t * H + 2 * ft:t * H + 2 * ft + 2, :], ident[:])
                last.then_inc(at_ps, 1)

            def project_out(b):
                pe.wait_ge(at_hi_done, b + 1)
                pe.wait_ge(at_lo_done, b + 1)
                for t in range(T):
                    for k in range(FT):
                        cols = slice(t * P, (t + 1) * P)
                        last = split_product(attn_ps[:, 3, t * D:(t + 1) * D], (at_hi[:, k, cols], at_lo[:, k, cols]),
                                             (w_hi[:, k, 3 * D:4 * D], w_lo[:, k, 3 * D:4 * D]), k == 0, k == FT - 1)
                last.then_inc(out_ps, 1)

            def transpose_x2(b, following):
                pe.wait_ge(x2_hat_done, b + 1)
                if following:
                    pe.wait_ge(q_norm_done, b + 2)
                for t in range(T):
                    for ft in range(FT):
                        last = nc.tensor.transpose(attn_ps[:, 3, ft * S + t * P:ft * S + (t + 1) * P],
                                                   x2_hat[:, t, ft * P:(ft + 1) * P], ident[:])
                last.then_inc(x2t_ps, 1)

            def router(b):
                pe.wait_ge(x2_hi_done, b + 1)
                pe.wait_ge(x2_lo_done, b + 1)
                for t in range(T):
                    for k in range(FT):
                        cols = slice(t * P, (t + 1) * P)
                        last = split_product(attn_ps[:, 3, t * E:(t + 1) * E], (x2_hi[:, k, cols], x2_lo[:, k, cols]),
                                             (gate_hi[:, k, :], gate_lo[:, k, :]), k == 0, k == FT - 1)
                last.then_inc(logit_ps, 1)

            def up(b, p, first):
                if first and p == 0:
                    pe.wait_ge(w_lo_done, 3)
                if p >= 2 or not first:
                    pe.wait_ge(relu_done, b * PAIRS + p - 1)
                for j in range(2):
                    for k in range(FT):
                        cols = slice((2 * p + j) * P, (2 * p + j + 1) * P)
                        last = split_product(up_ps[:, p % 2, j * S:(j + 1) * S], (up_hi[:, k, cols], up_lo[:, k, cols]),
                                             (x2_hi[:, k, :], x2_lo[:, k, :]), k == 0, k == FT - 1)
                last.then_inc(up_done, 1)

            def hidden(f, t):
                cols = slice((f % 2) * S + t * P, (f % 2) * S + (t + 1) * P)
                slot = (f // 2) % HID_RING
                return hid_hi[:, slot, cols], hid_lo[:, slot, cols]

            def down_shared(b, t, first):
                if t == 0:
                    pe.wait_ge(hid_hi_done, b * PAIRS + SP_PAIRS)
                    pe.wait_ge(hid_lo_done, b * PAIRS + SP_PAIRS)
                    if not first:
                        pe.wait_ge(acc_done, b * ACC)
                for f in range(FS):
                    last = split_product(down_ps[:, 0, t * D:(t + 1) * D], hidden(f, t),
                                         (down_hi[:, f, :], down_lo[:, f, :]), f == 0, f == FS - 1)
                if t == T - 1:
                    last.then_inc(down_done, 1)

            def down_expert(b, e, first):
                f = FS + e
                pe.wait_ge(hid_hi_done, b * PAIRS + f // 2 + 1)
                pe.wait_ge(hid_lo_done, b * PAIRS + f // 2 + 1)
                if e > 0:
                    pe.wait_ge(acc_done, b * ACC + 2 * e - 1)
                elif not first:
                    pe.wait_ge(acc_done, b * ACC - 2)
                for t in range(T):
                    last = split_product(down_ps[:, (e + 1) % 2, t * D:(t + 1) * D], hidden(f, t),
                                         (down_hi[:, f, :], down_lo[:, f, :]), True, True)
                last.then_inc(down_done, 1)

            def step(b, experts, following):
                first = isinstance(b, int) and b == 0
                f, f_first = (b - 1, isinstance(b, int) and b == 1)

                def ffn(what, n):
                    if experts:
                        if what == "up":
                            up(f, n, f_first)
                        elif what == "shared":
                            down_shared(f, n, f_first)
                        else:
                            down_expert(f, n, f_first)

                ffn("up", 0)
                ffn("up", 1)
                transpose_k(b)
                ffn("up", 2)
                scores(b, 0)
                scores(b, 1)
                ffn("shared", 0)
                scores(b, 2)
                scores(b, 3)
                ffn("shared", 1)
                scores(b, 4)
                scores(b, 5)
                ffn("up", 3)
                scores(b, 6)
                scores(b, 7)
                ffn("down", 0)
                fill = [("down", 1), ("up", 4), ("down", 2), ("down", 3), ("up", 5), ("down", 4), None, ("down", 5)]
                for u in range(U):
                    transpose_probs(b, u)
                    if fill[u]:
                        ffn(*fill[u])
                    if u:
                        probs_times_v(b, u - 1, first)
                probs_times_v(b, U - 1, first)
                if following:
                    transpose_ln(b + 1, False)
                ffn("down", 6)
                transpose_attn(b)
                ffn("down", 7)
                project_out(b)
                if following:
                    project_q(b + 1)
                    project_kv(b + 1, 1)
                    sum_q_squares(b + 1, False)
                    project_kv(b + 1, 2)
                transpose_x2(b, following)
                if following:
                    project_kv(b + 1, 0)
                router(b)

            pe.wait_ge(consts, 1)
            transpose_ln(0, True)
            pe.wait_ge(w_lo_done, 1)
            project_q(0)
            project_kv(0, 1)
            sum_q_squares(0, True)
            project_kv(0, 2)
            project_kv(0, 0)
            steps(pe, step)
            for p in range(3):
                up(B - 1, p, False)
            for t in range(T):
                down_shared(B - 1, t, False)
            up(B - 1, 3, False)
            down_expert(B - 1, 0, False)
            down_expert(B - 1, 1, False)
            up(B - 1, 4, False)
            down_expert(B - 1, 2, False)
            down_expert(B - 1, 3, False)
            up(B - 1, 5, False)
            for e in range(4, E):
                down_expert(B - 1, e, False)

        @block.scalar
        def _(act):
            def split_hi(n, dst, src):
                nc.scalar.activation(dst, src, ACT.Copy).then_inc(w_hi_done, 1)

            def ln_full(b, first):
                if not first:
                    act.wait_ge(ln_hi_done, b)
                    act.wait_ge(ln_lo_done, b)
                for ft in range(FT):
                    act.wait_ge(lnt_ps, b * FT + ft + 1)
                    for k, cols in enumerate((slice(0, S), slice(S, KEYS))):
                        last = nc.scalar.activation(ln_t[:, ft, cols], attn_ps[:, 1 + ft, cols], ACT.Identity,
                                                    bias=ln_b[:, k, ft:ft + 1], scale=ln_g[:, k, ft:ft + 1])
                last.then_inc(ln_full_done, 1)

            def q_out(b, first):
                act.wait_ge(q_ps, b + 1)
                if not first:
                    act.wait_ge(score_ps, b * U)
                    act.wait_ge(qn_ps, b)
                qv = attn_ps[:, 0, :].rearrange("p (f s) -> p f s", f=FT)
                nc.scalar.activation(q_hi[:], qv, ACT.Copy).then_inc(q_hi_done, 1)
                nc.scalar.activation(q_sq[:], qv, ACT.Square).then_inc(q_sq_done, 1)

            def kv_out(b, first):
                act.wait_ge(kv_ps, b * CH + CH)
                if not first:
                    act.wait_ge(k_sum_done, b)
                    act.wait_ge(pv_ps, b * U)
                nc.scalar.activation(k_sq[:], attn_ps[0:KC, 0:CH, 0:D], ACT.Square).then_inc(k_sq_done, 1)
                nc.scalar.activation(v_sb[:], attn_ps[0:KC, 0:CH, D:2 * D], ACT.Copy).then_inc(v_done, 1)

            def k_high(b, first):
                for ft in range(FT):
                    act.wait_ge(kt_ps, b * FT + ft + 1)
                    if not first:
                        act.wait_ge(score_ps, b * U)
                    nc.scalar.activation(k_hi[:, ft, 0:KEYS], attn_ps[:, ft, 0:KEYS], ACT.Copy,
                                         scale=gam_qk[:]).then_inc(k_hi_done, 1)

            def softmax(b, u, first):
                act.wait_ge(neg_max_done, b * T + u // H + 1)
                if not first:
                    act.wait_ge(pt_ps, b * U - U + u + 1)
                    act.wait_ge(row_inv_done, b)
                nc.scalar.activation(probs[:, u, :], masked[:, u, :], ACT.Exp, bias=neg_max[:, u:u + 1],
                                     scale=q_scale[:, u:u + 1], accum_out=row_sum[:, u:u + 1]).then_inc(prob_done, 1)

            def pt_out(b, u, first):
                act.wait_ge(pt_ps, b * U + u + 1)
                if not first or u >= PT_RING:
                    act.wait_ge(pv_ps, b * U + u + 1 - PT_RING)
                nc.scalar.activation(probs_t[:, u % PT_RING, :], attn_ps[0:KC, (u + 2) % 3, 0:CH * P],
                                     ACT.Copy).then_inc(pt_done, 1)

            def attn_high(b, first):
                act.wait_ge(at_ps, b + 1)
                if not first:
                    act.wait_ge(out_ps, b)
                nc.scalar.activation(at_hi[:], attn_ps[:, 0, :].rearrange("p (f s) -> p f s", f=FT),
                                     ACT.Copy).then_inc(at_hi_done, 1)

            def x2_high(b, first):
                act.wait_ge(x2t_ps, b + 1)
                if not first:
                    act.wait_ge(up_done, b * PAIRS)
                    act.wait_ge(logit_ps, b)
                nc.scalar.activation(x2_hi[:], attn_ps[:, 3, :].rearrange("p (f s) -> p f s", f=FT),
                                     ACT.Copy).then_inc(x2_hi_done, 1)

            def router_exp(b, first):
                act.wait_ge(logit_ps, b + 1)
                if not first:
                    act.wait_ge(router_step, (b - 1) * ROUTER_STEPS + 1)
                nc.scalar.activation(exp_neg[:], attn_ps[:, 3, 0:T * E].rearrange("p (t e) -> p t e", t=T),
                                     ACT.Exp, scale=-1.0).then_inc(exp_neg_done, 1)

            def hidden(b, p, first):
                act.wait_ge(up_done, b * PAIRS + p + 1)
                nc.scalar.activation(relu_sb[:, p % 2, :], up_ps[:, p % 2, :], ACT.Relu).then_inc(relu_done, 1)
                act.wait_ge(relu_done, b * PAIRS + p + 1)
                if not first or p >= 2:
                    act.wait_ge(hid_hi_done, b * PAIRS + p - 1)
                    act.wait_ge(hid_lo_done, b * PAIRS + p - 1)
                nc.scalar.activation(relu2[:, p % 2, :], relu_sb[:, p % 2, :], ACT.Square).then_inc(relu2_done, 1)

            def step(b, experts, following):
                first = isinstance(b, int) and b == 0
                f, f_first = b - 1, isinstance(b, int) and b == 1
                ffn = (lambda p: hidden(f, p, f_first)) if experts else (lambda p: None)
                kv_out(b, first)
                if first:
                    act.wait_ge(up_in, DMA)
                    split_hi(1, up_hi[:], up_stage[:])
                    act.wait_ge(down_in, DMA)
                    split_hi(2, down_hi[:], down_stage[:])
                ffn(0)
                ffn(1)
                k_high(b, first)
                ffn(2)
                for u in range(4):
                    softmax(b, u, first)
                ffn(3)
                for u in range(4, U):
                    softmax(b, u, first)
                for u in range(U):
                    pt_out(b, u, first)
                    if u == 2:
                        ffn(4)
                    if u == 5:
                        ffn(5)
                if following:
                    ln_full(b + 1, False)
                attn_high(b, first)
                if following:
                    q_out(b + 1, False)
                x2_high(b, first)
                router_exp(b, first)

            act.wait_ge(weights_in, 4 * DMA)
            nc.scalar.activation(gate_hi[:], gate_stage[:], ACT.Copy)
            split_hi(0, w_hi[:], w_stage[:])
            act.wait_ge(vectors_in, 10 * DMA)
            ln_full(0, True)
            q_out(0, True)
            steps(act, step)
            for p in range(PAIRS):
                hidden(B - 1, p, False)

        @block.vector
        def _(dve):
            def carry():
                nc.vector.memset(carrier[:], 0.0)

            def layer_norm1(b, first):
                k = b * LN1_STEPS
                dve.wait_ge(x_loaded, b * DMA + DMA)
                for t in range(T):
                    nc.vector.bn_stats(stats1[:, t, :], x_in[:, t, :]).then_inc(ln1_step, 1)
                dve.wait_ge(c_loaded, b * DMA + DMA)
                nc.vector.bn_stats(stats1[0:C, T, :], c_in[:]).then_inc(ln1_step, 1)
                dve.wait_ge(mask_loaded, b * DMA + DMA)
                if not first:
                    dve.wait_ge(mask_done, b)
                dve.wait_ge(ln1_step, k + T + 1)
                nc.vector.tensor_scalar(mask_row[:, S:KEYS], mask_in[:], -1.0, MASKED, ALU.add, ALU.mult).then_inc(mask_done, 1)
                if first:
                    dve.wait_ge(zeroed, 1)
                for t in range(T + 1):
                    rows = P if t < T else C
                    nc.vector.bn_aggr(mv1[0:rows, t, :], stats1[0:rows, t, :]).then_inc(ln1_step, 1)
                dve.wait_ge(ln1_step, k + LN1_STEPS)
                if not first:
                    dve.wait_ge(rstd1_done, b)
                nc.vector.tensor_scalar(var1[:, 0:T], mv1[:, 0:T, 1], 1.0 + LN_EPS, LN_EPS * LN_EPS, ALU.mult, ALU.add)
                nc.vector.tensor_scalar(var1[0:C, T:T + 1], mv1[0:C, T, 1:2], LN_EPS, None, ALU.add).then_inc(var1_done, 1)

            def normalize1(b, first):
                dve.wait_ge(rstd1_done, b + 1)
                if not first:
                    dve.wait_ge(lnt_ps, b * FT)
                for t in range(T):
                    nc.vector.tensor_scalar(x_hat[:, t, :], x_in[:, t, :], mv1[:, t, 0:1], rstd1[:, t:t + 1],
                                            ALU.subtract, ALU.mult)
                nc.vector.tensor_scalar(c_hat[:], c_in[:], mv1[0:C, T, 0:1], rstd1[0:C, T:T + 1],
                                        ALU.subtract, ALU.mult).then_inc(x_hat_done, 1)

            def ln_high(b, first):
                dve.wait_ge(ln_full_done, b + 1)
                if not first:
                    dve.wait_ge(kv_ps, b * CH)
                nc.vector.tensor_copy(ln_hi[:], ln_t[:]).then_inc(ln_hi_done, 1)

            def q_low(b):
                dve.wait_ge(q_hi_done, b + 1)
                dve.wait_ge(q_sq_done, b + 1)
                nc.vector.tensor_tensor(q_lo[:], attn_ps[:, 0, :].rearrange("p (f s) -> p f s", f=FT), q_hi[:],
                                        ALU.subtract).then_inc(q_lo_done, 1)

            def q_norms(b, first):
                dve.wait_ge(qn_ps, b + 1)
                if not first:
                    dve.wait_ge(q_scale_done, b)
                nc.vector.tensor_scalar(q_norm[:], attn_ps[:, 3, 0:U], DH * RMS_EPS * RMS_EPS, None,
                                        ALU.max).then_inc(q_norm_done, 1)

            def k_norms(b, first):
                dve.wait_ge(k_sq_done, b + 1)
                nc.vector.tensor_reduce(k_sum[:], k_sq[:].rearrange("p c (h d) -> p (c h) d", d=DH), AX_X,
                                        ALU.add).then_inc(k_sum_done, 1)
                dve.wait_ge(k_sum_done, b + 1)
                if not first:
                    dve.wait_ge(k_scale_done, b)
                nc.vector.tensor_scalar(k_norm[:], k_sum[:], 1.0 / DH, RMS_EPS * RMS_EPS, ALU.mult,
                                        ALU.max).then_inc(k_norm_done, 1)

            def k_normalize(b, first):
                dve.wait_ge(k_scale_done, b + 1)
                dve.wait_ge(v_done, b + 1)
                if not first:
                    dve.wait_ge(kt_ps, b * FT)
                for c in range(CH):
                    last = nc.vector.tensor_tensor(
                        k_rms[:, c, :].rearrange("p (h d) -> p h d", d=DH),
                        attn_ps[0:KC, c, 0:D].rearrange("p (h d) -> p h d", d=DH),
                        k_scale[:, c * H:(c + 1) * H].unsqueeze(2).to_broadcast([KC, H, DH]), ALU.mult)
                last.then_inc(k_rms_done, 1)

            def k_low(b):
                for ft in range(FT):
                    dve.wait_ge(k_hi_done, b * FT + ft + 1)
                    nc.vector.scalar_tensor_tensor(k_lo[:, ft, 0:KEYS], attn_ps[:, ft, 0:KEYS], gam_qk[:],
                                                   k_hi[:, ft, 0:KEYS], ALU.mult, ALU.subtract).then_inc(k_lo_done, 1)

            def mask_scores(b, u, first):
                if u % 2 == 0:
                    dve.wait_ge(score_ps, b * U + u + 2)
                    if not first:
                        dve.wait_ge(prob_done, b * U - U + u + 2)
                    if u == 0:
                        dve.wait_ge(mask_done, b + 1)
                    carry()
                nc.vector.tensor_tensor_reduce(masked[:, u, :], attn_ps[:, u % 3, 0:KEYS], mask_row[:], 1.0, -MASKED,
                                               ALU.add, ALU.max, row_max[:, u:u + 1]).then_inc(masked_done, 1)

            def negate_max(b, t):
                cols = slice(t * H, (t + 1) * H)
                dve.wait_ge(masked_done, b * U + (t + 1) * H)
                dve.wait_ge(q_scale_done, b + 1)
                nc.vector.scalar_tensor_tensor(neg_max[:, cols], row_max[:, cols], -1.0, q_scale[:, cols],
                                               ALU.mult, ALU.mult).then_inc(neg_max_done, 1)

            def attn_out(b, first):
                dve.wait_ge(prob_done, b * U + U)
                nc.vector.reciprocal(row_inv[:], row_sum[:]).then_inc(row_inv_done, 1)
                dve.wait_ge(row_inv_done, b + 1)
                dve.wait_ge(pv_ps, b * U + U)
                if not first:
                    dve.wait_ge(at_ps, b)
                nc.vector.tensor_tensor(attn[:], attn_ps[:, 3, :].rearrange("p (u d) -> p u d", d=DH),
                                        row_inv[:].unsqueeze(2).to_broadcast([P, U, DH]), ALU.mult).then_inc(attn_done, 1)

            def attn_low(b):
                dve.wait_ge(at_hi_done, b + 1)
                nc.vector.tensor_tensor(at_lo[:], attn_ps[:, 0, :].rearrange("p (f s) -> p f s", f=FT), at_hi[:],
                                        ALU.subtract).then_inc(at_lo_done, 1)

            def layer_norm2(b, first):
                k = b * LN2_STEPS
                dve.wait_ge(out_ps, b + 1)
                dve.wait_ge(x_res_done, b + 1)
                nc.vector.tensor_tensor(x1[:], attn_ps[:, 3, :].rearrange("p (t d) -> p t d", d=D), x_res[:],
                                        ALU.add).then_inc(x1_done, 1)
                dve.wait_ge(x1_done, b + 1)
                for t in range(T):
                    nc.vector.bn_stats(stats2[:, t, :], x1[:, t, :]).then_inc(ln2_step, 1)
                dve.wait_ge(ln2_step, k + T)
                carry()
                for t in range(T):
                    nc.vector.bn_aggr(mv2[:, t, :], stats2[:, t, :]).then_inc(ln2_step, 1)
                dve.wait_ge(ln2_step, k + LN2_STEPS)
                if not first:
                    dve.wait_ge(rstd2_done, b)
                nc.vector.tensor_scalar(var2[:], mv2[:, :, 1], LN_EPS, None, ALU.add).then_inc(var2_done, 1)

            def normalize2(b, first):
                dve.wait_ge(rstd2_done, b + 1)
                if not first:
                    dve.wait_ge(x2t_ps, b)
                for t in range(T):
                    last = nc.vector.tensor_scalar(x2_hat[:, t, :], x1[:, t, :], mv2[:, t, 0:1], rstd2[:, t:t + 1],
                                                   ALU.subtract, ALU.mult)
                last.then_inc(x2_hat_done, 1)

            def x2_low(b):
                dve.wait_ge(x2_hi_done, b + 1)
                nc.vector.tensor_tensor(x2_lo[:], attn_ps[:, 3, :].rearrange("p (f s) -> p f s", f=FT), x2_hi[:],
                                        ALU.subtract).then_inc(x2_lo_done, 1)

            def route(b):
                k = b * ROUTER_STEPS
                n = [0]

                def then(ins, needs=None):
                    n[0] += 1
                    ins.then_inc(router_step, 1)

                def after(count):
                    dve.wait_ge(router_step, k + count)

                dve.wait_ge(exp_neg_done, b + 1)
                then(nc.vector.tensor_scalar(sig_den[:], exp_neg[:], 1.0, None, ALU.add))
                after(1)
                then(nc.vector.reciprocal(score[:], sig_den[:]))
                after(2)
                then(nc.vector.tensor_tensor(biased[:], score[:], gbias[:].unsqueeze(1).to_broadcast([P, T, E]), ALU.add))
                after(3)
                quad = biased[:].rearrange("p t (g a c) -> p (t g) a c", a=2, c=2)
                then(nc.vector.tensor_tensor(pair_hi[:], quad[:, :, :, 0], quad[:, :, :, 1], ALU.max))
                then(nc.vector.tensor_tensor(pair_lo[:], quad[:, :, :, 0], quad[:, :, :, 1], ALU.min))
                after(5)
                then(nc.vector.tensor_tensor(top1[:], pair_hi[:, :, 0], pair_hi[:, :, 1], ALU.max))
                then(nc.vector.tensor_tensor(mid_a[:], pair_hi[:, :, 0], pair_hi[:, :, 1], ALU.min))
                then(nc.vector.tensor_tensor(mid_b[:], pair_lo[:, :, 0], pair_lo[:, :, 1], ALU.max))
                after(8)
                then(nc.vector.tensor_tensor(top2[:], mid_a[:], mid_b[:], ALU.max))
                after(9)
                then(nc.vector.tensor_tensor(group_sum[:].rearrange("p t g -> p (t g)"), top1[:], top2[:], ALU.add))
                after(10)
                then(nc.vector.tensor_tensor(group_sel[:, :, 0], group_sum[:, :, 0], group_sum[:, :, 1], ALU.is_ge))
                then(nc.vector.tensor_tensor(group_sel[:, :, 1], group_sum[:, :, 0], group_sum[:, :, 1], ALU.is_lt))
                after(12)
                then(nc.vector.tensor_tensor(in_group[:].rearrange("p t (g q) -> p (t g) q", g=G),
                                             biased[:].rearrange("p t (g q) -> p (t g) q", g=G),
                                             group_sel[:].rearrange("p t g -> p (t g)").unsqueeze(2).to_broadcast([P, T * G, E // G]),
                                             ALU.mult))
                after(13)
                other = in_group[:].unsqueeze(2).to_broadcast([P, T, E, E])
                own = in_group[:].unsqueeze(3).to_broadcast([P, T, E, E])
                then(nc.vector.tensor_tensor(above[:], other, own, ALU.is_gt))
                then(nc.vector.tensor_tensor(tied[:], other, own, ALU.is_equal))
                after(15)
                then(nc.vector.tensor_tensor(tied_low[:], tied[:], lower[:].unsqueeze(1).to_broadcast([P, T, E, E]), ALU.mult))
                after(16)
                then(nc.vector.tensor_tensor(beats[:], above[:], tied_low[:], ALU.add))
                after(17)
                then(nc.vector.tensor_reduce(rank[:], beats[:], AX_X, ALU.add))
                after(18)
                then(nc.vector.scalar_tensor_tensor(picked[:], rank[:], 2.0, score[:], ALU.is_lt, ALU.mult))
                after(19)
                then(nc.vector.tensor_reduce(pick_sum[:], picked[:], AX_X, ALU.add))
                after(20)
                then(nc.vector.tensor_scalar(pick_eps[:], pick_sum[:], 1e-20, None, ALU.add))
                after(21)
                then(nc.vector.reciprocal(pick_inv[:], pick_eps[:]))
                after(22)
                then(nc.vector.scalar_tensor_tensor(route_w[:], picked[:], ROUTED_SCALE,
                                                    pick_inv[:].unsqueeze(2).to_broadcast([P, T, E]),
                                                    ALU.mult, ALU.mult))
                assert n[0] == ROUTER_STEPS

            def hidden_high(b, p, first):
                dve.wait_ge(relu2_done, b * PAIRS + p + 1)
                used = {0: -4, 1: -2, 2: 0, 3: 1, 4: 1, 5: 3}[p]
                if p >= HID_RING or not first:
                    dve.wait_ge(down_done, b * (E + 1) + used)
                nc.vector.tensor_copy(hid_hi[:, p % HID_RING, :], relu2[:, p % 2, :]).then_inc(hid_hi_done, 1)

            def add_shared(b, first):
                dve.wait_ge(down_done, b * (E + 1) + 1)
                if not first:
                    dve.wait_ge(stored, b * DMA)
                nc.vector.tensor_tensor(acc[:], down_ps[:, 0, :].rearrange("p (t d) -> p t d", d=D), x1[:],
                                        ALU.add).then_inc(acc_done, 1)

            def add_expert(b, e):
                dve.wait_ge(down_done, b * (E + 1) + e + 2)
                if e == 0:
                    dve.wait_ge(router_step, b * ROUTER_STEPS + ROUTER_STEPS)
                for t in range(T):
                    dve.wait_ge(acc_done, b * ACC + (2 * e + t if e else 1))
                    nc.vector.scalar_tensor_tensor(acc[:, t, :], down_ps[:, (e + 1) % 2, t * D:(t + 1) * D],
                                                   route_w[:, t, e:e + 1], acc[:, t, :], ALU.mult,
                                                   ALU.add).then_inc(acc_done, 1)

            def split_lo(dst, src, hi):
                nc.vector.tensor_tensor(dst, src, hi, ALU.subtract).then_inc(w_lo_done, 1)

            def step(b, experts, following):
                first = isinstance(b, int) and b == 0
                f, f_first = b - 1, isinstance(b, int) and b == 1

                def high(p):
                    if experts:
                        hidden_high(f, p, f_first)

                def add(e):
                    if experts:
                        add_expert(f, e)

                k_norms(b, first)
                if experts:
                    route(f)
                k_normalize(b, first)
                high(0)
                high(1)
                k_low(b)
                high(2)
                for u in range(4):
                    mask_scores(b, u, first)
                negate_max(b, 0)
                if experts:
                    add_shared(f, f_first)
                for u in range(4, U):
                    mask_scores(b, u, first)
                negate_max(b, 1)
                if first:
                    dve.wait_ge(w_hi_done, 2)
                    split_lo(up_lo[:], up_stage[:], up_hi[:])
                    dve.wait_ge(w_hi_done, 3)
                    split_lo(down_lo[:], down_stage[:], down_hi[:])
                high(3)
                add(0)
                if following:
                    layer_norm1(b + 1, False)
                add(1)
                high(4)
                add(2)
                if following:
                    normalize1(b + 1, False)
                add(3)
                high(5)
                add(4)
                add(5)
                attn_out(b, first)
                if following:
                    ln_high(b + 1, False)
                add(6)
                attn_low(b)
                add(7)
                layer_norm2(b, first)
                if following:
                    q_low(b + 1)
                    q_norms(b + 1, False)
                normalize2(b, first)
                x2_low(b)

            for h in range(2):
                for block_head in range(2):
                    last = nc.vector.memset(head_sel[h * DH:(h + 1) * DH, block_head:block_head + 1], float(h == block_head))
            last.then_inc(head_sel_done, 1)
            layer_norm1(0, True)
            dve.wait_ge(vectors_in, 10 * DMA)
            nc.vector.tensor_tensor(gam_qk[:], gam_q[:], gam_k[:], ALU.mult).then_inc(gamma_done, 1)
            normalize1(0, True)
            dve.wait_ge(w_hi_done, 1)
            nc.vector.tensor_tensor(gate_lo[:], gate_stage[:], gate_hi[:], ALU.subtract)
            split_lo(w_lo[:], w_stage[:], w_hi[:])
            ln_high(0, True)
            q_low(0)
            q_norms(0, True)
            dve.wait_ge(gamma_done, 1)
            steps(dve, step)
            f = B - 1
            route(f)
            for p in range(3):
                hidden_high(f, p, False)
            add_shared(f, False)
            hidden_high(f, 3, False)
            add_expert(f, 0)
            add_expert(f, 1)
            hidden_high(f, 4, False)
            add_expert(f, 2)
            add_expert(f, 3)
            hidden_high(f, 5, False)
            for e in range(4, E):
                add_expert(f, e)

        @block.gpsimd
        def _(pool):
            def inverse_root(dst, src, done):
                nc.gpsimd.tensor_tensor(dst, src, minus_half[0:src.shape[0], 0:src.shape[1]], ALU.pow).then_inc(done, 1)

            def rstd_first(b, first):
                pool.wait_ge(var1_done, b + 1)
                if not first:
                    pool.wait_ge(x_hat_done, b)
                inverse_root(rstd1[:], var1[:], rstd1_done)

            def ln_low(b):
                pool.wait_ge(ln_hi_done, b + 1)
                nc.gpsimd.tensor_tensor(ln_lo[:], ln_t[:], ln_hi[:], ALU.subtract).then_inc(ln_lo_done, 1)

            def residual(b, first):
                pool.wait_ge(x_loaded, b * DMA + DMA)
                if not first:
                    pool.wait_ge(x1_done, b)
                nc.gpsimd.tensor_tensor(x_res[:], x_in[:], bout_row[:].unsqueeze(1).to_broadcast([P, T, D]),
                                        ALU.add).then_inc(x_res_done, 1)

            def q_scales(b, first):
                pool.wait_ge(q_norm_done, b + 1)
                if not first:
                    pool.wait_ge(prob_done, b * U)
                inverse_root(q_scale[:], q_norm[:], q_scale_done)

            def k_scales(b, first):
                pool.wait_ge(k_norm_done, b + 1)
                if not first:
                    pool.wait_ge(k_rms_done, b)
                inverse_root(k_scale[:], k_norm[:], k_scale_done)

            def rstd_second(b, first):
                pool.wait_ge(var2_done, b + 1)
                if not first:
                    pool.wait_ge(x2_hat_done, b)
                inverse_root(rstd2[:], var2[:], rstd2_done)

            def hidden_low(b, p):
                pool.wait_ge(hid_hi_done, b * PAIRS + p + 1)
                nc.gpsimd.tensor_tensor(hid_lo[:, p % HID_RING, :], relu2[:, p % 2, :], hid_hi[:, p % HID_RING, :],
                                        ALU.subtract).then_inc(hid_lo_done, 1)

            def step(b, experts, following):
                first = isinstance(b, int) and b == 0

                def low(p):
                    if experts:
                        hidden_low(b - 1, p)

                k_scales(b, first)
                for p in range(4):
                    low(p)
                if following:
                    rstd_first(b + 1, False)
                low(4)
                low(5)
                if following:
                    ln_low(b + 1)
                rstd_second(b, first)
                if following:
                    q_scales(b + 1, False)
                    residual(b + 1, False)

            for dst, src in ((ln_g[:, 0, :], g_l), (ln_g[:, 1, :], g_x), (ln_b[:, 0, :], b_l), (ln_b[:, 1, :], b_x)):
                pool.dma_start(dst, src).then_inc(vectors_in, DMA)
            for h in range(2):
                rows = slice(h * DH, (h + 1) * DH)
                pool.dma_start(gam_q[rows, :], q_gamma.rearrange("(d a) -> d a", a=1)).then_inc(vectors_in, DMA)
                pool.dma_start(gam_k[rows, :], k_gamma.rearrange("(d a) -> d a", a=1)).then_inc(vectors_in, DMA)
            pool.dma_start(bout_row[:], b_out.partition_broadcast(P)).then_inc(vectors_in, DMA)
            pool.dma_start(gbias[:], gate_bias.partition_broadcast(P)).then_inc(vectors_in, DMA)
            nc.gpsimd.memset(minus_half[:], -0.5)
            nc.gpsimd.memset(mask_row[:, 0:S], 0.0)
            nc.gpsimd.memset(k_hi[:, :, KEYS:KPAD].bitcast(F32), 0.0)
            nc.gpsimd.memset(k_lo[:, :, KEYS:KPAD].bitcast(F32), 0.0)
            nc.gpsimd.memset(var1[:], 1.0).then_inc(zeroed, 1)
            nc.gpsimd.memset(ident[:], 0.0)
            nc.gpsimd.memset(lower[:], 0.0).then_inc(zeroed, 1)
            pool.wait_ge(zeroed, 2)
            for e in range(1, E):
                nc.gpsimd.memset(lower[:, e, 0:e], 1.0)
            nc.gpsimd.affine_select(out=ident[:], in_=ident[:], compare_op=ALU.not_equal, fill=1.0, base=0,
                                    pattern=[[-1, P]], channel_multiplier=1).then_inc(consts, 1)
            rstd_first(0, True)
            pool.wait_ge(vectors_in, 10 * DMA)
            residual(0, True)
            ln_low(0)
            q_scales(0, True)
            steps(pool, step)
            for p in range(PAIRS):
                hidden_low(B - 1, p)


_INS = ["x", "ctx", "mask", "g_x", "b_x", "g_l", "b_l", "q_gamma", "k_gamma", "w_q", "w_kv", "w_out", "b_out",
        "gate_t", "gate_bias", "up_t", "down_t"]


def kernel(x, ctx_1024, mask_BxS2_bk0, L0_xattn_ln_x_g, L0_xattn_ln_x_b, L0_xattn_ln_l_g, L0_xattn_ln_l_b,
           L0_xattn_q_gamma, L0_xattn_k_gamma, L0_xattn_W_q, L0_xattn_W_kv, L0_xattn_W_out, L0_xattn_b_out,
           L0_ffn_gate_weight, L0_ffn_gate_bias, L0_ffn_up_weights, L0_ffn_down_weights,
           L0_ffn_shared_up_weight, L0_ffn_shared_down_weight):
    import numpy as np
    import concourse.bacc as bacc
    from concourse.bass_utils import run_bass_kernel_spmd

    x = np.ascontiguousarray(x)
    up, down = np.asarray(L0_ffn_up_weights), np.asarray(L0_ffn_down_weights)
    experts, inner, dim = up.shape
    up_t = np.concatenate([np.asarray(L0_ffn_shared_up_weight), up.reshape(experts * inner, dim)], axis=0).T
    down_t = np.concatenate([np.asarray(L0_ffn_shared_down_weight).T,
                             down.transpose(0, 2, 1).reshape(experts * inner, dim)], axis=0)
    columns = [np.asarray(v).reshape(-1, 128).T for v in (L0_xattn_ln_x_g, L0_xattn_ln_x_b,
                                                         L0_xattn_ln_l_g, L0_xattn_ln_l_b)]
    given = [x, ctx_1024, mask_BxS2_bk0, *columns, L0_xattn_q_gamma, L0_xattn_k_gamma, L0_xattn_W_q, L0_xattn_W_kv,
             L0_xattn_W_out, L0_xattn_b_out, np.asarray(L0_ffn_gate_weight).T, L0_ffn_gate_bias, up_t, down_t]

    nc = bacc.Bacc("TRN2", target_bir_lowering=False, num_devices=1)
    arrays, args = {}, []
    for name, a in zip(_INS, given):
        a = np.ascontiguousarray(a)
        arrays[f"in_{name}"] = a
        args.append(nc.dram_tensor(f"in_{name}", a.shape, mybir.dt.from_np(a.dtype), kind="ExternalInput").ap())
    out = nc.dram_tensor("out", x.shape, mybir.dt.float32, kind="ExternalOutput").ap()
    build(nc, *args, out)
    r = run_bass_kernel_spmd(nc, [arrays], core_ids=[0])
    return r.results[0]["out"]
```

```python
from contextlib import ExitStack

import concourse.bass as bass
from concourse import mybir

F32 = mybir.dt.float32
F32R = mybir.dt.float32r
U8 = mybir.dt.uint8
ALU = mybir.AluOpType
ACT = mybir.ActivationFunctionType
AX_X = mybir.AxisListType.X

LN_EPS = 1e-5
RMS_EPS = 1e-8
MASKED = 3.0e38
ROUTED_SCALE = 2.5
DMA = 16


def build(nc, x, ctx_in, mask, g_x, b_x, g_l, b_l, q_gamma, k_gamma, w_q, w_kv, w_out, b_out,
          gate_t, gate_bias, up_t, down_t, out):
    B, S, D = x.shape
    C = ctx_in.shape[1]
    P = 128
    DH = q_gamma.shape[0]
    H = D // DH
    T = S // P
    FT = D // P
    KEYS = S + C
    CH = 3
    KC = KEYS // CH
    KPAD = KEYS + KEYS % 2
    E = gate_t.shape[1]
    F = up_t.shape[1] // P
    FS = F - E
    PAIRS = F // 2
    SP_PAIRS = FS // 2
    U = T * H
    G = E // 4
    assert KC * CH == KEYS and KC <= P and D == 256 and S == 256 and 2 * DH == P and FS == 4
    ACC = 1 + 2 * E

    with ExitStack() as stack:
        def sb(name, shape, dt=F32):
            return stack.enter_context(nc.sbuf_tensor(name, shape, dt))

        def sem(name):
            return stack.enter_context(nc.semaphore(name))

        ident = sb("ident", [P, P])
        head_sel = sb("head_sel", [P, 2])
        lower = sb("lower", [P, E, E])
        minus_half = sb("minus_half", [P, 16])
        ln_g = sb("ln_g", [P, 2, FT])
        ln_b = sb("ln_b", [P, 2, FT])
        gam_q = sb("gam_q", [P, 1])
        gam_k = sb("gam_k", [P, 1])
        gam_qk = sb("gam_qk", [P, 1])
        bout_row = sb("bout_row", [P, D])
        gbias = sb("gbias", [P, E])
        w_stage = sb("w_stage", [P, FT, 4 * D])
        up_stage = sb("up_stage", [P, FT, F * P])
        down_stage = sb("down_stage", [P, F, D])
        gate_stage = sb("gate_stage", [P, FT, E])
        w_hi, w_lo = sb("w_hi", [P, FT, 4 * D], F32R), sb("w_lo", [P, FT, 4 * D], F32R)
        up_hi, up_lo = sb("up_hi", [P, FT, F * P], F32R), sb("up_lo", [P, FT, F * P], F32R)
        down_hi, down_lo = sb("down_hi", [P, F, D], F32R), sb("down_lo", [P, F, D], F32R)
        gate_hi, gate_lo = sb("gate_hi", [P, FT, E], F32R), sb("gate_lo", [P, FT, E], F32R)

        x_in = sb("x_in", [P, T, D])
        c_in = sb("c_in", [C, D])
        mask_in = sb("mask_in", [P, C], U8)
        mask_row = sb("mask_row", [P, KEYS])
        x_res = sb("x_res", [P, T, D])
        stats1 = sb("stats1", [P, T + 1, 6])
        mv1 = sb("mv1", [P, T + 1, 2])
        var1 = sb("var1", [P, T + 1])
        rstd1 = sb("rstd1", [P, T + 1])
        x_hat = sb("x_hat", [P, T, D])
        c_hat = sb("c_hat", [C, D])
        ln_t = sb("ln_t", [P, FT, KEYS])
        ln_hi, ln_lo = sb("ln_hi", [P, FT, KEYS], F32R), sb("ln_lo", [P, FT, KEYS], F32R)
        q_hi, q_lo = sb("q_hi", [P, FT, S], F32R), sb("q_lo", [P, FT, S], F32R)
        q_sq = sb("q_sq", [P, FT, S])
        q_norm = sb("q_norm", [P, U])
        q_scale = sb("q_scale", [P, U])
        k_sq = sb("k_sq", [KC, CH, D])
        k_sum = sb("k_sum", [KC, CH * H])
        k_norm = sb("k_norm", [KC, CH * H])
        k_scale = sb("k_scale", [KC, CH * H])
        k_rms = sb("k_rms", [KC, CH, D])
        v_sb = sb("v_sb", [KC, CH, D])
        k_hi, k_lo = sb("k_hi", [P, FT, KPAD], F32R), sb("k_lo", [P, FT, KPAD], F32R)

        masked = sb("masked", [P, U, KEYS])
        row_max = sb("row_max", [P, U])
        neg_max = sb("neg_max", [P, U])
        probs = sb("probs", [P, U, KEYS])
        row_sum = sb("row_sum", [P, U])
        row_inv = sb("row_inv", [P, U])
        PT_RING = 3
        probs_t = sb("probs_t", [KC, PT_RING, CH * P])
        attn = sb("attn", [P, U, DH])
        at_hi, at_lo = sb("at_hi", [P, FT, S], F32R), sb("at_lo", [P, FT, S], F32R)
        x1 = sb("x1", [P, T, D])
        stats2 = sb("stats2", [P, T, 6])
        mv2 = sb("mv2", [P, T, 2])
        var2 = sb("var2", [P, T])
        rstd2 = sb("rstd2", [P, T])
        x2_hat = sb("x2_hat", [P, T, D])
        x2_hi, x2_lo = sb("x2_hi", [P, FT, S], F32R), sb("x2_lo", [P, FT, S], F32R)

        exp_neg = sb("exp_neg", [P, T, E])
        sig_den = sb("sig_den", [P, T, E])
        score = sb("score", [P, T, E])
        biased = sb("biased", [P, T, E])
        pair_hi = sb("pair_hi", [P, T * G, 2])
        pair_lo = sb("pair_lo", [P, T * G, 2])
        top1 = sb("top1", [P, T * G])
        mid_a = sb("mid_a", [P, T * G])
        mid_b = sb("mid_b", [P, T * G])
        top2 = sb("top2", [P, T * G])
        group_sum = sb("group_sum", [P, T, G])
        group_sel = sb("group_sel", [P, T, G])
        in_group = sb("in_group", [P, T, E])
        above = sb("above", [P, T, E, E])
        tied = sb("tied", [P, T, E, E])
        tied_low = sb("tied_low", [P, T, E, E])
        beats = sb("beats", [P, T, E, E])
        rank = sb("rank", [P, T, E])
        picked = sb("picked", [P, T, E])
        pick_sum = sb("pick_sum", [P, T])
        pick_eps = sb("pick_eps", [P, T])
        pick_inv = sb("pick_inv", [P, T])
        route_w = sb("route_w", [P, T, E])
        relu_sb = sb("relu_sb", [P, 2, 2 * S])
        relu2 = sb("relu2", [P, 2, 2 * S])
        HID_RING = 3
        hid_hi = sb("hid_hi", [P, HID_RING, 2 * S], F32R)
        hid_lo = sb("hid_lo", [P, HID_RING, 2 * S], F32R)
        acc = sb("acc", [P, T, D])
        carrier = sb("carrier", [P, 1])

        attn_ps = stack.enter_context(nc.psum_tensor("attn_ps", [P, 4, 512], F32))
        up_ps = stack.enter_context(nc.psum_tensor("up_ps", [P, 2, 512], F32))
        down_ps = stack.enter_context(nc.psum_tensor("down_ps", [P, 2, 512], F32))

        weights_in, up_in, down_in = sem("weights_in"), sem("up_in"), sem("down_in")
        vectors_in = sem("vectors_in")
        x_loaded, c_loaded, mask_loaded = sem("x_loaded"), sem("c_loaded"), sem("mask_loaded")
        stored = sem("stored")
        consts, zeroed = sem("consts"), sem("zeroed")
        w_hi_done, w_lo_done = sem("w_hi_done"), sem("w_lo_done")
        gamma_done, head_sel_done = sem("gamma_done"), sem("head_sel_done")
        lnt_ps, q_ps, kv_ps, qn_ps, kt_ps = sem("lnt_ps"), sem("q_ps"), sem("kv_ps"), sem("qn_ps"), sem("kt_ps")
        score_ps, pt_ps, pv_ps = sem("score_ps"), sem("pt_ps"), sem("pv_ps")
        at_ps, out_ps, x2t_ps, logit_ps = sem("at_ps"), sem("out_ps"), sem("x2t_ps"), sem("logit_ps")
        up_done, down_done = sem("up_done"), sem("down_done")
        ln_full_done = sem("ln_full_done")
        q_hi_done, q_sq_done = sem("q_hi_done"), sem("q_sq_done")
        k_sq_done, v_done, k_hi_done = sem("k_sq_done"), sem("v_done"), sem("k_hi_done")
        prob_done, pt_done = sem("prob_done"), sem("pt_done")
        at_hi_done, x2_hi_done, exp_neg_done = sem("at_hi_done"), sem("x2_hi_done"), sem("exp_neg_done")
        relu_done, relu2_done = sem("relu_done"), sem("relu2_done")
        ln1_step, var1_done, x_hat_done, mask_done = sem("ln1_step"), sem("var1_done"), sem("x_hat_done"), sem("mask_done")
        ln_hi_done, q_lo_done, q_norm_done = sem("ln_hi_done"), sem("q_lo_done"), sem("q_norm_done")
        k_sum_done, k_norm_done, k_rms_done, k_lo_done = sem("k_sum_done"), sem("k_norm_done"), sem("k_rms_done"), sem("k_lo_done")
        masked_done, neg_max_done = sem("masked_done"), sem("neg_max_done")
        row_inv_done, attn_done, at_lo_done, x1_done = sem("row_inv_done"), sem("attn_done"), sem("at_lo_done"), sem("x1_done")
        ln2_step, var2_done, x2_hat_done, x2_lo_done = sem("ln2_step"), sem("var2_done"), sem("x2_hat_done"), sem("x2_lo_done")
        router_step, hid_hi_done, acc_done = sem("router_step"), sem("hid_hi_done"), sem("acc_done")
        rstd1_done, ln_lo_done, x_res_done = sem("rstd1_done"), sem("ln_lo_done"), sem("x_res_done")
        q_scale_done, k_scale_done, rstd2_done, hid_lo_done = sem("q_scale_done"), sem("k_scale_done"), sem("rstd2_done"), sem("hid_lo_done")

        PARTS = (slice(1, 3), slice(0, 1))
        LN1_STEPS = 2 * (T + 1)
        LN2_STEPS = 2 * T
        ROUTER_STEPS = 23

        block = stack.enter_context(nc.Block())

        def steps(eng, step):
            step(0, False, True)
            step(1, True, True)
            with eng.Fori(2, B - 1) as b:
                step(b, True, True)
            step(B - 1, True, False)

        @block.sync
        def _(sp):
            def load(b, first):
                if not first:
                    sp.wait_ge(x_hat_done, b)
                    sp.wait_ge(x_res_done, b)
                    sp.wait_ge(mask_done, b)
                sp.dma_start(x_in[:], x[b].rearrange("(t p) d -> p t d", p=P)).then_inc(x_loaded, DMA)
                sp.dma_start(c_in[:], ctx_in[b]).then_inc(c_loaded, DMA)
                sp.dma_start(mask_in[:], mask[b].partition_broadcast(P)).then_inc(mask_loaded, DMA)

            def store(b):
                sp.wait_ge(acc_done, b * ACC + ACC)
                sp.dma_start(out[b].rearrange("(t p) d -> p t d", p=P), acc[:]).then_inc(stored, DMA)

            load(0, True)
            sp.dma_start(w_stage[:, :, 0:D], w_q.rearrange("(k p) n -> p k n", p=P)).then_inc(weights_in, DMA)
            sp.dma_start(w_stage[:, :, D:3 * D], w_kv.rearrange("(k p) n -> p k n", p=P)).then_inc(weights_in, DMA)
            sp.dma_start(w_stage[:, :, 3 * D:4 * D], w_out.rearrange("(k p) n -> p k n", p=P)).then_inc(weights_in, DMA)
            sp.dma_start(gate_stage[:], gate_t.rearrange("(k p) n -> p k n", p=P)).then_inc(weights_in, DMA)
            sp.dma_start(up_stage[:], up_t.rearrange("(k p) n -> p k n", p=P)).then_inc(up_in, DMA)
            sp.dma_start(down_stage[:], down_t.rearrange("(f p) n -> p f n", p=P)).then_inc(down_in, DMA)
            load(1, False)

            def step(b, experts, following):
                if following and not (isinstance(b, int) and b == 0):
                    load(b + 1, False)
                if experts:
                    store(b - 1)

            steps(sp, step)
            store(B - 1)
            sp.wait_ge(stored, B * DMA)

        @block.tensor
        def _(pe):
            def split_product(out_ap, stationary, moving, first, last):
                (s_hi, s_lo), (m_hi, m_lo) = stationary, moving
                nc.tensor.matmul(out_ap, s_hi, m_hi, start=first, stop=False)
                nc.tensor.matmul(out_ap, s_hi, m_lo, start=False, stop=False)
                return nc.tensor.matmul(out_ap, s_lo, m_hi, start=False, stop=last)

            def transpose_ln(b, first):
                pe.wait_ge(x_hat_done, b + 1)
                for ft in range(FT):
                    if not first:
                        pe.wait_ge(pt_done, b * U - (2 if ft == 0 else 1))
                    for t in range(T):
                        nc.tensor.transpose(attn_ps[:, 1 + ft, t * P:(t + 1) * P], x_hat[:, t, ft * P:(ft + 1) * P], ident[:])
                    nc.tensor.transpose(attn_ps[:, 1 + ft, S:KEYS], c_hat[:, ft * P:(ft + 1) * P],
                                        ident[0:C, 0:C]).then_inc(lnt_ps, 1)

            def project_q(b, experts):
                if not (isinstance(b, int) and b == 0):
                    pe.wait_ge(q_norm_done, b)
                if experts:
                    pe.wait_ge(acc_done, (b - 2) * ACC + ACC - 2)
                for ft in range(FT):
                    for k in range(FT):
                        cols = slice(ft * P, (ft + 1) * P)
                        last = split_product(down_ps[:, 1, ft * S:(ft + 1) * S],
                                             (w_hi[:, k, cols], w_lo[:, k, cols]),
                                             (ln_hi[:, k, 0:S], ln_lo[:, k, 0:S]), k == 0, k == FT - 1)
                last.then_inc(q_ps, 1)

            def project_kv(b, c):
                if c == 1:
                    pe.wait_ge(ln_hi_done, b + 1)
                    pe.wait_ge(ln_lo_done, b + 1)
                rows = slice(c * KC, (c + 1) * KC)
                for k in range(FT):
                    last = split_product(attn_ps[0:KC, c, :], (ln_hi[:, k, rows], ln_lo[:, k, rows]),
                                         (w_hi[:, k, D:3 * D], w_lo[:, k, D:3 * D]), k == 0, k == FT - 1)
                last.then_inc(kv_ps, 1)

            def sum_q_squares(b, first):
                pe.wait_ge(q_sq_done, b + 1)
                pe.wait_ge(q_lo_done, b + 1)
                if first:
                    pe.wait_ge(head_sel_done, 1)
                for t in range(T):
                    for ft in range(FT):
                        last = nc.tensor.matmul(down_ps[:, 1, t * H + 2 * ft:t * H + 2 * ft + 2],
                                                q_sq[:, ft, t * P:(t + 1) * P], head_sel[:], start=True, stop=True)
                last.then_inc(qn_ps, 1)

            def transpose_k(b):
                pe.wait_ge(k_rms_done, b * CH + CH)
                pe.wait_ge(v_done, b + 1)
                for ft in range(FT):
                    for c in range(CH):
                        last = nc.tensor.transpose(attn_ps[:, ft, c * KC:(c + 1) * KC],
                                                   k_rms[:, c, ft * P:(ft + 1) * P], ident[0:KC, 0:KC])
                    last.then_inc(kt_ps, 1)

            def scores(b, u):
                t, h = divmod(u, H)
                if u < 2:
                    pe.wait_ge(k_hi_done, b * FT + u + 1)
                    pe.wait_ge(k_lo_done, b * FT + u + 1)
                elif u >= 3:
                    pe.wait_ge(masked_done, b * U + u - 2)
                ft, rows = h // 2, slice((h % 2) * DH, (h % 2 + 1) * DH)
                cols = slice(t * P, (t + 1) * P)
                split_product(attn_ps[:, u % 3, 0:KPAD], (q_hi[rows, ft, cols], q_lo[rows, ft, cols]),
                              (k_hi[rows, ft, :], k_lo[rows, ft, :]), True, True).then_inc(score_ps, 1)

            def transpose_probs(b, u):
                pe.wait_ge(prob_done, b * U + u + 1)
                if u < 3:
                    pe.wait_ge(masked_done, b * U + 6 + u)
                else:
                    pe.wait_ge(pt_done, b * U + u - 2)
                for c in range(CH):
                    last = nc.tensor.transpose(attn_ps[0:KC, (u + 2) % 3, c * P:(c + 1) * P],
                                               probs[:, u, c * KC:(c + 1) * KC], ident[:])
                last.then_inc(pt_ps, 1)

            def probs_times_v(b, u, first):
                if u == 0:
                    if not first:
                        pe.wait_ge(x2_lo_done, b)
                        pe.wait_ge(exp_neg_done, b)
                pe.wait_ge(pt_done, b * U + u + 1)
                h = u % H
                for c in range(CH):
                    last = nc.tensor.matmul(attn_ps[:, 3, u * DH:(u + 1) * DH],
                                            probs_t[:, u % PT_RING, c * P:(c + 1) * P],
                                            v_sb[:, c, h * DH:(h + 1) * DH], start=(c == 0), stop=(c == CH - 1))
                last.then_inc(pv_ps, 1)

            def transpose_attn(b):
                pe.wait_ge(attn_done, b + 1)
                pe.wait_ge(pt_done, b * U + U)
                for t in range(T):
                    for ft in range(FT):
                        last = nc.tensor.transpose(attn_ps[:, 0, ft * S + t * P:ft * S + (t + 1) * P],
                                                   attn[:, t * H + 2 * ft:t * H + 2 * ft + 2, :], ident[:])
                last.then_inc(at_ps, 1)

            def project_out(b):
                pe.wait_ge(at_hi_done, b + 1)
                pe.wait_ge(at_lo_done, b + 1)
                for t in range(T):
                    for k in range(FT):
                        cols = slice(t * P, (t + 1) * P)
                        last = split_product(attn_ps[:, 3, t * D:(t + 1) * D], (at_hi[:, k, cols], at_lo[:, k, cols]),
                                             (w_hi[:, k, 3 * D:4 * D], w_lo[:, k, 3 * D:4 * D]), k == 0, k == FT - 1)
                last.then_inc(out_ps, 1)

            def transpose_x2(b):
                pe.wait_ge(x2_hat_done, b + 1)
                for t in range(T):
                    for ft in range(FT):
                        last = nc.tensor.transpose(attn_ps[:, 3, ft * S + t * P:ft * S + (t + 1) * P],
                                                   x2_hat[:, t, ft * P:(ft + 1) * P], ident[:])
                last.then_inc(x2t_ps, 1)

            def router(b):
                pe.wait_ge(x2_hi_done, b + 1)
                pe.wait_ge(x2_lo_done, b + 1)
                for t in range(T):
                    for k in range(FT):
                        cols = slice(t * P, (t + 1) * P)
                        last = split_product(attn_ps[:, 3, t * E:(t + 1) * E], (x2_hi[:, k, cols], x2_lo[:, k, cols]),
                                             (gate_hi[:, k, :], gate_lo[:, k, :]), k == 0, k == FT - 1)
                last.then_inc(logit_ps, 1)

            def up(b, p, first):
                if first and p == 0:
                    pe.wait_ge(w_lo_done, 3)
                if p == 0:
                    pe.wait_ge(x2_hi_done, b + 1)
                    pe.wait_ge(x2_lo_done, b + 1)
                if p >= 2 or not first:
                    pe.wait_ge(relu_done, b * PAIRS + p - 1)
                for j in range(2):
                    for k in range(FT):
                        cols = slice((2 * p + j) * P, (2 * p + j + 1) * P)
                        last = split_product(up_ps[:, p % 2, j * S:(j + 1) * S], (up_hi[:, k, cols], up_lo[:, k, cols]),
                                             (x2_hi[:, k, :], x2_lo[:, k, :]), k == 0, k == FT - 1)
                last.then_inc(up_done, 1)

            def hidden(f, t):
                cols = slice((f % 2) * S + t * P, (f % 2) * S + (t + 1) * P)
                slot = (f // 2) % HID_RING
                return hid_hi[:, slot, cols], hid_lo[:, slot, cols]

            def down_shared(b, t, first):
                if t == 0:
                    pe.wait_ge(hid_hi_done, b * PAIRS + SP_PAIRS)
                    pe.wait_ge(hid_lo_done, b * PAIRS + SP_PAIRS)
                    if not first:
                        pe.wait_ge(acc_done, b * ACC)
                for f in range(FS):
                    last = split_product(down_ps[:, 0, t * D:(t + 1) * D], hidden(f, t),
                                         (down_hi[:, f, :], down_lo[:, f, :]), f == 0, f == FS - 1)
                if t == T - 1:
                    last.then_inc(down_done, 1)

            def down_expert(b, e, first, following=True):
                f = FS + e
                if e == 0 and following:
                    pe.wait_ge(q_norm_done, b + 2)
                pe.wait_ge(hid_hi_done, b * PAIRS + f // 2 + 1)
                pe.wait_ge(hid_lo_done, b * PAIRS + f // 2 + 1)
                if e > 0:
                    pe.wait_ge(acc_done, b * ACC + 2 * e - 1)
                elif not first:
                    pe.wait_ge(acc_done, b * ACC - 2)
                for t in range(T):
                    last = split_product(down_ps[:, (e + 1) % 2, t * D:(t + 1) * D], hidden(f, t),
                                         (down_hi[:, f, :], down_lo[:, f, :]), True, True)
                last.then_inc(down_done, 1)

            def step(b, experts, following):
                first = isinstance(b, int) and b == 0
                f, f_first = (b - 1, isinstance(b, int) and b == 1)

                def ffn(what, n):
                    if experts:
                        if what == "up":
                            up(f, n, f_first)
                        elif what == "shared":
                            down_shared(f, n, f_first)
                        else:
                            down_expert(f, n, f_first)

                ffn("up", 0)
                sum_q_squares(b, first)
                if experts:
                    router(f)
                transpose_k(b)
                ffn("up", 1)
                ffn("up", 2)
                for u in range(4):
                    scores(b, u)
                ffn("shared", 0)
                scores(b, 4)
                scores(b, 5)
                ffn("shared", 1)
                scores(b, 6)
                scores(b, 7)
                ffn("up", 3)
                transpose_probs(b, 0)
                ffn("down", 0)
                transpose_probs(b, 1)
                probs_times_v(b, 0, first)
                ffn("down", 1)
                transpose_probs(b, 2)
                probs_times_v(b, 1, first)
                ffn("up", 4)
                transpose_probs(b, 3)
                probs_times_v(b, 2, first)
                ffn("down", 2)
                transpose_probs(b, 4)
                probs_times_v(b, 3, first)
                ffn("up", 5)
                transpose_probs(b, 5)
                probs_times_v(b, 4, first)
                ffn("down", 3)
                transpose_probs(b, 6)
                probs_times_v(b, 5, first)
                ffn("down", 4)
                transpose_probs(b, 7)
                probs_times_v(b, 6, first)
                if following:
                    transpose_ln(b + 1, False)
                probs_times_v(b, 7, first)
                ffn("down", 5)
                transpose_attn(b)
                ffn("down", 6)
                ffn("down", 7)
                project_out(b)
                if following:
                    project_kv(b + 1, 1)
                    project_kv(b + 1, 2)
                    project_kv(b + 1, 0)
                transpose_x2(b)
                if following:
                    project_q(b + 1, experts)

            pe.wait_ge(consts, 1)
            transpose_ln(0, True)
            pe.wait_ge(w_lo_done, 1)
            project_kv(0, 1)
            project_kv(0, 2)
            project_kv(0, 0)
            project_q(0, False)
            steps(pe, step)
            up(B - 1, 0, False)
            router(B - 1)
            up(B - 1, 1, False)
            up(B - 1, 2, False)
            for t in range(T):
                down_shared(B - 1, t, False)
            up(B - 1, 3, False)
            down_expert(B - 1, 0, False, False)
            down_expert(B - 1, 1, False)
            up(B - 1, 4, False)
            down_expert(B - 1, 2, False)
            down_expert(B - 1, 3, False)
            up(B - 1, 5, False)
            for e in range(4, E):
                down_expert(B - 1, e, False)

        @block.scalar
        def _(act):
            def split_hi(n, dst, src):
                nc.scalar.activation(dst, src, ACT.Copy).then_inc(w_hi_done, 1)

            def ln_full(b, first):
                if not first:
                    act.wait_ge(ln_hi_done, b)
                    act.wait_ge(ln_lo_done, b)
                for ft in range(FT):
                    act.wait_ge(lnt_ps, b * FT + ft + 1)
                    for k, cols in enumerate((slice(0, S), slice(S, KEYS))):
                        last = nc.scalar.activation(ln_t[:, ft, cols], attn_ps[:, 1 + ft, cols], ACT.Identity,
                                                    bias=ln_b[:, k, ft:ft + 1], scale=ln_g[:, k, ft:ft + 1])
                last.then_inc(ln_full_done, 1)

            def q_out(b, first):
                act.wait_ge(q_ps, b + 1)
                if not first:
                    act.wait_ge(score_ps, b * U)
                    act.wait_ge(qn_ps, b)
                qv = down_ps[:, 1, :].rearrange("p (f s) -> p f s", f=FT)
                nc.scalar.activation(q_hi[:], qv, ACT.Copy).then_inc(q_hi_done, 1)
                nc.scalar.activation(q_sq[:], qv, ACT.Square).then_inc(q_sq_done, 1)

            def k_squares(b, part, first):
                act.wait_ge(kv_ps, b * CH + 2 + part)
                if not first:
                    act.wait_ge(k_sum_done, b * 2)
                nc.scalar.activation(k_sq[:, PARTS[part], :], attn_ps[0:KC, PARTS[part], 0:D],
                                     ACT.Square).then_inc(k_sq_done, 1)

            def v_out(b, first):
                if not first:
                    act.wait_ge(pv_ps, b * U)
                nc.scalar.activation(v_sb[:], attn_ps[0:KC, 0:CH, D:2 * D], ACT.Copy).then_inc(v_done, 1)

            def k_high(b, first):
                for ft in range(FT):
                    act.wait_ge(kt_ps, b * FT + ft + 1)
                    if not first:
                        act.wait_ge(score_ps, b * U)
                    nc.scalar.activation(k_hi[:, ft, 0:KEYS], attn_ps[:, ft, 0:KEYS], ACT.Copy,
                                         scale=gam_qk[:]).then_inc(k_hi_done, 1)

            def softmax(b, u, first):
                act.wait_ge(neg_max_done, b * T + u // H + 1)
                if not first:
                    act.wait_ge(pt_ps, b * U - U + u + 1)
                    act.wait_ge(row_inv_done, b)
                nc.scalar.activation(probs[:, u, :], masked[:, u, :], ACT.Exp, bias=neg_max[:, u:u + 1],
                                     scale=q_scale[:, u:u + 1], accum_out=row_sum[:, u:u + 1]).then_inc(prob_done, 1)

            def pt_out(b, u, first):
                act.wait_ge(pt_ps, b * U + u + 1)
                if not first or u >= PT_RING:
                    act.wait_ge(pv_ps, b * U + u + 1 - PT_RING)
                nc.scalar.activation(probs_t[:, u % PT_RING, :], attn_ps[0:KC, (u + 2) % 3, 0:CH * P],
                                     ACT.Copy).then_inc(pt_done, 1)

            def attn_high(b, first):
                act.wait_ge(at_ps, b + 1)
                if not first:
                    act.wait_ge(out_ps, b)
                nc.scalar.activation(at_hi[:], attn_ps[:, 0, :].rearrange("p (f s) -> p f s", f=FT),
                                     ACT.Copy).then_inc(at_hi_done, 1)

            def x2_high(b, first):
                act.wait_ge(x2t_ps, b + 1)
                if not first:
                    act.wait_ge(up_done, b * PAIRS)
                nc.scalar.activation(x2_hi[:], attn_ps[:, 3, :].rearrange("p (f s) -> p f s", f=FT),
                                     ACT.Copy).then_inc(x2_hi_done, 1)

            def router_exp(b, first):
                act.wait_ge(logit_ps, b + 1)
                if not first:
                    act.wait_ge(router_step, (b - 1) * ROUTER_STEPS + 1)
                nc.scalar.activation(exp_neg[:], attn_ps[:, 3, 0:T * E].rearrange("p (t e) -> p t e", t=T),
                                     ACT.Exp, scale=-1.0).then_inc(exp_neg_done, 1)

            def hidden(b, p, first):
                act.wait_ge(up_done, b * PAIRS + p + 1)
                nc.scalar.activation(relu_sb[:, p % 2, :], up_ps[:, p % 2, :], ACT.Relu).then_inc(relu_done, 1)
                act.wait_ge(relu_done, b * PAIRS + p + 1)
                if not first or p >= 2:
                    act.wait_ge(hid_hi_done, b * PAIRS + p - 1)
                    act.wait_ge(hid_lo_done, b * PAIRS + p - 1)
                nc.scalar.activation(relu2[:, p % 2, :], relu_sb[:, p % 2, :], ACT.Square).then_inc(relu2_done, 1)

            def step(b, experts, following):
                first = isinstance(b, int) and b == 0
                f, f_first = b - 1, isinstance(b, int) and b == 1
                ffn = (lambda p: hidden(f, p, f_first)) if experts else (lambda p: None)
                if first:
                    act.wait_ge(up_in, DMA)
                    split_hi(1, up_hi[:], up_stage[:])
                ffn(0)
                if experts:
                    router_exp(f, f_first)
                k_high(b, first)
                if first:
                    act.wait_ge(down_in, DMA)
                    split_hi(2, down_hi[:], down_stage[:])
                ffn(1)
                ffn(2)
                for u in range(4):
                    softmax(b, u, first)
                softmax(b, 4, first)
                ffn(3)
                pt_out(b, 0, first)
                softmax(b, 5, first)
                pt_out(b, 1, first)
                softmax(b, 6, first)
                softmax(b, 7, first)
                pt_out(b, 2, first)
                ffn(4)
                pt_out(b, 3, first)
                pt_out(b, 4, first)
                ffn(5)
                for u in range(5, U):
                    pt_out(b, u, first)
                if following:
                    ln_full(b + 1, False)
                attn_high(b, first)
                if following:
                    k_squares(b + 1, 0, False)
                    k_squares(b + 1, 1, False)
                x2_high(b, first)
                if following:
                    v_out(b + 1, False)
                    q_out(b + 1, False)

            act.wait_ge(weights_in, 4 * DMA)
            nc.scalar.activation(gate_hi[:], gate_stage[:], ACT.Copy)
            split_hi(0, w_hi[:], w_stage[:])
            act.wait_ge(vectors_in, 10 * DMA)
            ln_full(0, True)
            k_squares(0, 0, True)
            k_squares(0, 1, True)
            v_out(0, True)
            q_out(0, True)
            steps(act, step)
            hidden(B - 1, 0, False)
            router_exp(B - 1, False)
            for p in range(1, PAIRS):
                hidden(B - 1, p, False)

        @block.vector
        def _(dve):
            def carry():
                nc.vector.memset(carrier[:], 0.0)

            def layer_norm1(b, first):
                k = b * LN1_STEPS
                dve.wait_ge(x_loaded, b * DMA + DMA)
                for t in range(T):
                    nc.vector.bn_stats(stats1[:, t, :], x_in[:, t, :]).then_inc(ln1_step, 1)
                dve.wait_ge(c_loaded, b * DMA + DMA)
                nc.vector.bn_stats(stats1[0:C, T, :], c_in[:]).then_inc(ln1_step, 1)
                dve.wait_ge(mask_loaded, b * DMA + DMA)
                if not first:
                    dve.wait_ge(mask_done, b)
                dve.wait_ge(ln1_step, k + T + 1)
                nc.vector.tensor_scalar(mask_row[:, S:KEYS], mask_in[:], -1.0, MASKED, ALU.add, ALU.mult).then_inc(mask_done, 1)
                if first:
                    dve.wait_ge(zeroed, 1)
                for t in range(T + 1):
                    rows = P if t < T else C
                    nc.vector.bn_aggr(mv1[0:rows, t, :], stats1[0:rows, t, :]).then_inc(ln1_step, 1)
                dve.wait_ge(ln1_step, k + LN1_STEPS)
                if not first:
                    dve.wait_ge(rstd1_done, b)
                nc.vector.tensor_scalar(var1[:, 0:T], mv1[:, 0:T, 1], 1.0 + LN_EPS, LN_EPS * LN_EPS, ALU.mult, ALU.add)
                nc.vector.tensor_scalar(var1[0:C, T:T + 1], mv1[0:C, T, 1:2], LN_EPS, None, ALU.add).then_inc(var1_done, 1)

            def normalize1(b, first):
                dve.wait_ge(rstd1_done, b + 1)
                if not first:
                    dve.wait_ge(lnt_ps, b * FT)
                for t in range(T):
                    nc.vector.tensor_scalar(x_hat[:, t, :], x_in[:, t, :], mv1[:, t, 0:1], rstd1[:, t:t + 1],
                                            ALU.subtract, ALU.mult)
                nc.vector.tensor_scalar(c_hat[:], c_in[:], mv1[0:C, T, 0:1], rstd1[0:C, T:T + 1],
                                        ALU.subtract, ALU.mult).then_inc(x_hat_done, 1)

            def ln_high(b, first):
                dve.wait_ge(ln_full_done, b + 1)
                if not first:
                    dve.wait_ge(kv_ps, b * CH)
                nc.vector.tensor_copy(ln_hi[:], ln_t[:]).then_inc(ln_hi_done, 1)

            def q_low(b):
                dve.wait_ge(q_hi_done, b + 1)
                dve.wait_ge(q_sq_done, b + 1)
                nc.vector.tensor_tensor(q_lo[:], down_ps[:, 1, :].rearrange("p (f s) -> p f s", f=FT), q_hi[:],
                                        ALU.subtract).then_inc(q_lo_done, 1)

            def q_norms(b, first):
                dve.wait_ge(qn_ps, b + 1)
                if not first:
                    dve.wait_ge(q_scale_done, b)
                nc.vector.tensor_scalar(q_norm[:], down_ps[:, 1, 0:U], DH * RMS_EPS * RMS_EPS, None,
                                        ALU.max).then_inc(q_norm_done, 1)

            def k_norms(b, part, first):
                cs = PARTS[part]
                cols = slice(cs.start * H, cs.stop * H)
                dve.wait_ge(k_sq_done, b * 2 + part + 1)
                nc.vector.tensor_reduce(k_sum[:, cols], k_sq[:, cs, :].rearrange("p c (h d) -> p (c h) d", d=DH), AX_X,
                                        ALU.add).then_inc(k_sum_done, 1)
                dve.wait_ge(k_sum_done, b * 2 + part + 1)
                if not first:
                    dve.wait_ge(k_scale_done, b * 2)
                nc.vector.tensor_scalar(k_norm[:, cols], k_sum[:, cols], 1.0 / DH, RMS_EPS * RMS_EPS, ALU.mult,
                                        ALU.max).then_inc(k_norm_done, 1)

            def k_normalize(b, part, first):
                dve.wait_ge(k_scale_done, b * 2 + part + 1)
                dve.wait_ge(v_done, b + 1)
                if not first:
                    dve.wait_ge(kt_ps, b * FT)
                for c in range(PARTS[part].start, PARTS[part].stop):
                    nc.vector.tensor_tensor(
                        k_rms[:, c, :].rearrange("p (h d) -> p h d", d=DH),
                        attn_ps[0:KC, c, 0:D].rearrange("p (h d) -> p h d", d=DH),
                        k_scale[:, c * H:(c + 1) * H].unsqueeze(2).to_broadcast([KC, H, DH]),
                        ALU.mult).then_inc(k_rms_done, 1)

            def k_low(b, ft):
                dve.wait_ge(k_hi_done, b * FT + ft + 1)
                nc.vector.scalar_tensor_tensor(k_lo[:, ft, 0:KEYS], attn_ps[:, ft, 0:KEYS], gam_qk[:],
                                               k_hi[:, ft, 0:KEYS], ALU.mult, ALU.subtract).then_inc(k_lo_done, 1)

            def mask_scores(b, u, first):
                if u % 2 == 0:
                    dve.wait_ge(score_ps, b * U + u + 2)
                    if not first:
                        dve.wait_ge(prob_done, b * U - U + u + 2)
                    if u == 0:
                        dve.wait_ge(mask_done, b + 1)
                    carry()
                nc.vector.tensor_tensor_reduce(masked[:, u, :], attn_ps[:, u % 3, 0:KEYS], mask_row[:], 1.0, -MASKED,
                                               ALU.add, ALU.max, row_max[:, u:u + 1]).then_inc(masked_done, 1)

            def negate_max(b, t):
                cols = slice(t * H, (t + 1) * H)
                dve.wait_ge(masked_done, b * U + (t + 1) * H)
                dve.wait_ge(q_scale_done, b + 1)
                nc.vector.scalar_tensor_tensor(neg_max[:, cols], row_max[:, cols], -1.0, q_scale[:, cols],
                                               ALU.mult, ALU.mult).then_inc(neg_max_done, 1)

            def invert_sums(b):
                dve.wait_ge(prob_done, b * U + U)
                nc.vector.reciprocal(row_inv[:], row_sum[:]).then_inc(row_inv_done, 1)

            def attn_out(b, first):
                dve.wait_ge(row_inv_done, b + 1)
                dve.wait_ge(pv_ps, b * U + U)
                if not first:
                    dve.wait_ge(at_ps, b)
                nc.vector.tensor_tensor(attn[:], attn_ps[:, 3, :].rearrange("p (u d) -> p u d", d=DH),
                                        row_inv[:].unsqueeze(2).to_broadcast([P, U, DH]), ALU.mult).then_inc(attn_done, 1)

            def attn_low(b):
                dve.wait_ge(at_hi_done, b + 1)
                nc.vector.tensor_tensor(at_lo[:], attn_ps[:, 0, :].rearrange("p (f s) -> p f s", f=FT), at_hi[:],
                                        ALU.subtract).then_inc(at_lo_done, 1)

            def layer_norm2(b, first):
                k = b * LN2_STEPS
                dve.wait_ge(out_ps, b + 1)
                dve.wait_ge(x_res_done, b + 1)
                nc.vector.tensor_tensor(x1[:], attn_ps[:, 3, :].rearrange("p (t d) -> p t d", d=D), x_res[:],
                                        ALU.add).then_inc(x1_done, 1)
                dve.wait_ge(x1_done, b + 1)
                for t in range(T):
                    nc.vector.bn_stats(stats2[:, t, :], x1[:, t, :]).then_inc(ln2_step, 1)
                dve.wait_ge(ln2_step, k + T)
                carry()
                for t in range(T):
                    nc.vector.bn_aggr(mv2[:, t, :], stats2[:, t, :]).then_inc(ln2_step, 1)
                dve.wait_ge(ln2_step, k + LN2_STEPS)
                if not first:
                    dve.wait_ge(rstd2_done, b)
                nc.vector.tensor_scalar(var2[:], mv2[:, :, 1], LN_EPS, None, ALU.add).then_inc(var2_done, 1)

            def normalize2(b, first):
                dve.wait_ge(rstd2_done, b + 1)
                if not first:
                    dve.wait_ge(x2t_ps, b)
                for t in range(T):
                    last = nc.vector.tensor_scalar(x2_hat[:, t, :], x1[:, t, :], mv2[:, t, 0:1], rstd2[:, t:t + 1],
                                                   ALU.subtract, ALU.mult)
                last.then_inc(x2_hat_done, 1)

            def x2_low(b):
                dve.wait_ge(x2_hi_done, b + 1)
                nc.vector.tensor_tensor(x2_lo[:], attn_ps[:, 3, :].rearrange("p (f s) -> p f s", f=FT), x2_hi[:],
                                        ALU.subtract).then_inc(x2_lo_done, 1)

            def route(b, *levels):
                for level in levels:
                    route_level(b, level)

            def route_level(b, level):
                upto = (0, 1, 2, 3, 5, 8, 9, 10, 12, 13, 15, 16, 17, 18, 19, 20, 21, 22, 23)
                quad = biased[:].rearrange("p t (g a c) -> p (t g) a c", a=2, c=2)
                other = in_group[:].unsqueeze(2).to_broadcast([P, T, E, E])
                own = in_group[:].unsqueeze(3).to_broadcast([P, T, E, E])
                if level == 1:
                    dve.wait_ge(exp_neg_done, b + 1)
                else:
                    dve.wait_ge(router_step, b * ROUTER_STEPS + upto[level - 1])
                if level == 1:
                    nc.vector.tensor_scalar(sig_den[:], exp_neg[:], 1.0, None, ALU.add).then_inc(router_step, 1)
                elif level == 2:
                    nc.vector.reciprocal(score[:], sig_den[:]).then_inc(router_step, 1)
                elif level == 3:
                    nc.vector.tensor_tensor(biased[:], score[:], gbias[:].unsqueeze(1).to_broadcast([P, T, E]),
                                            ALU.add).then_inc(router_step, 1)
                elif level == 4:
                    nc.vector.tensor_tensor(pair_hi[:], quad[:, :, :, 0], quad[:, :, :, 1], ALU.max).then_inc(router_step, 1)
                    nc.vector.tensor_tensor(pair_lo[:], quad[:, :, :, 0], quad[:, :, :, 1], ALU.min).then_inc(router_step, 1)
                elif level == 5:
                    nc.vector.tensor_tensor(top1[:], pair_hi[:, :, 0], pair_hi[:, :, 1], ALU.max).then_inc(router_step, 1)
                    nc.vector.tensor_tensor(mid_a[:], pair_hi[:, :, 0], pair_hi[:, :, 1], ALU.min).then_inc(router_step, 1)
                    nc.vector.tensor_tensor(mid_b[:], pair_lo[:, :, 0], pair_lo[:, :, 1], ALU.max).then_inc(router_step, 1)
                elif level == 6:
                    nc.vector.tensor_tensor(top2[:], mid_a[:], mid_b[:], ALU.max).then_inc(router_step, 1)
                elif level == 7:
                    nc.vector.tensor_tensor(group_sum[:].rearrange("p t g -> p (t g)"), top1[:], top2[:],
                                            ALU.add).then_inc(router_step, 1)
                elif level == 8:
                    nc.vector.tensor_tensor(group_sel[:, :, 0], group_sum[:, :, 0], group_sum[:, :, 1],
                                            ALU.is_ge).then_inc(router_step, 1)
                    nc.vector.tensor_tensor(group_sel[:, :, 1], group_sum[:, :, 0], group_sum[:, :, 1],
                                            ALU.is_lt).then_inc(router_step, 1)
                elif level == 9:
                    nc.vector.tensor_tensor(in_group[:].rearrange("p t (g q) -> p (t g) q", g=G),
                                            biased[:].rearrange("p t (g q) -> p (t g) q", g=G),
                                            group_sel[:].rearrange("p t g -> p (t g)").unsqueeze(2)
                                            .to_broadcast([P, T * G, E // G]), ALU.mult).then_inc(router_step, 1)
                elif level == 10:
                    nc.vector.tensor_tensor(above[:], other, own, ALU.is_gt).then_inc(router_step, 1)
                    nc.vector.tensor_tensor(tied[:], other, own, ALU.is_equal).then_inc(router_step, 1)
                elif level == 11:
                    nc.vector.tensor_tensor(tied_low[:], tied[:], lower[:].unsqueeze(1).to_broadcast([P, T, E, E]),
                                            ALU.mult).then_inc(router_step, 1)
                elif level == 12:
                    nc.vector.tensor_tensor(beats[:], above[:], tied_low[:], ALU.add).then_inc(router_step, 1)
                elif level == 13:
                    nc.vector.tensor_reduce(rank[:], beats[:], AX_X, ALU.add).then_inc(router_step, 1)
                elif level == 14:
                    nc.vector.scalar_tensor_tensor(picked[:], rank[:], 2.0, score[:], ALU.is_lt,
                                                   ALU.mult).then_inc(router_step, 1)
                elif level == 15:
                    nc.vector.tensor_reduce(pick_sum[:], picked[:], AX_X, ALU.add).then_inc(router_step, 1)
                elif level == 16:
                    nc.vector.tensor_scalar(pick_eps[:], pick_sum[:], 1e-20, None, ALU.add).then_inc(router_step, 1)
                elif level == 17:
                    nc.vector.reciprocal(pick_inv[:], pick_eps[:]).then_inc(router_step, 1)
                elif level == 18:
                    nc.vector.scalar_tensor_tensor(route_w[:], picked[:], ROUTED_SCALE,
                                                   pick_inv[:].unsqueeze(2).to_broadcast([P, T, E]),
                                                   ALU.mult, ALU.mult).then_inc(router_step, 1)

            def hidden_high(b, p, first):
                dve.wait_ge(relu2_done, b * PAIRS + p + 1)
                used = {0: -4, 1: -2, 2: 0, 3: 1, 4: 1, 5: 3}[p]
                if p >= HID_RING or not first:
                    dve.wait_ge(down_done, b * (E + 1) + used)
                nc.vector.tensor_copy(hid_hi[:, p % HID_RING, :], relu2[:, p % 2, :]).then_inc(hid_hi_done, 1)

            def add_shared(b, first):
                dve.wait_ge(down_done, b * (E + 1) + 1)
                if not first:
                    dve.wait_ge(stored, b * DMA)
                nc.vector.tensor_tensor(acc[:], down_ps[:, 0, :].rearrange("p (t d) -> p t d", d=D), x1[:],
                                        ALU.add).then_inc(acc_done, 1)

            def add_expert(b, e):
                dve.wait_ge(down_done, b * (E + 1) + e + 2)
                if e == 0:
                    dve.wait_ge(router_step, b * ROUTER_STEPS + ROUTER_STEPS)
                for t in range(T):
                    dve.wait_ge(acc_done, b * ACC + (2 * e + t if e else 1))
                    nc.vector.scalar_tensor_tensor(acc[:, t, :], down_ps[:, (e + 1) % 2, t * D:(t + 1) * D],
                                                   route_w[:, t, e:e + 1], acc[:, t, :], ALU.mult,
                                                   ALU.add).then_inc(acc_done, 1)

            def split_lo(dst, src, hi):
                nc.vector.tensor_tensor(dst, src, hi, ALU.subtract).then_inc(w_lo_done, 1)

            def step(b, experts, following):
                first = isinstance(b, int) and b == 0
                f, f_first = b - 1, isinstance(b, int) and b == 1

                def high(p):
                    if experts:
                        hidden_high(f, p, f_first)

                def add(e):
                    if experts:
                        add_expert(f, e)

                def routing(*levels):
                    if experts:
                        route(f, *levels)

                k_normalize(b, 0, first)
                q_low(b)
                k_normalize(b, 1, first)
                high(0)
                q_norms(b, first)
                routing(1)
                k_low(b, 0)
                routing(2)
                k_low(b, 1)
                routing(3)
                if first:
                    dve.wait_ge(w_hi_done, 2)
                    split_lo(up_lo[:], up_stage[:], up_hi[:])
                    dve.wait_ge(w_hi_done, 3)
                    split_lo(down_lo[:], down_stage[:], down_hi[:])
                high(1)
                routing(4)
                high(2)
                routing(5)
                mask_scores(b, 0, first)
                mask_scores(b, 1, first)
                routing(6)
                mask_scores(b, 2, first)
                mask_scores(b, 3, first)
                routing(7)
                negate_max(b, 0)
                routing(8, 9, 10)
                mask_scores(b, 4, first)
                mask_scores(b, 5, first)
                routing(11, 12)
                if experts:
                    add_shared(f, f_first)
                routing(13)
                mask_scores(b, 6, first)
                mask_scores(b, 7, first)
                routing(14)
                negate_max(b, 1)
                routing(15, 16)
                if following:
                    layer_norm1(b + 1, False)
                routing(17)
                high(3)
                routing(18)
                add(0)
                if following:
                    normalize1(b + 1, False)
                add(1)
                high(4)
                add(2)
                high(5)
                add(3)
                invert_sums(b)
                add(4)
                attn_out(b, first)
                add(5)
                if following:
                    ln_high(b + 1, False)
                attn_low(b)
                add(6)
                layer_norm2(b, first)
                add(7)
                normalize2(b, first)
                if following:
                    k_norms(b + 1, 0, False)
                    k_norms(b + 1, 1, False)
                x2_low(b)

            for h in range(2):
                for block_head in range(2):
                    last = nc.vector.memset(head_sel[h * DH:(h + 1) * DH, block_head:block_head + 1], float(h == block_head))
            last.then_inc(head_sel_done, 1)
            layer_norm1(0, True)
            dve.wait_ge(vectors_in, 10 * DMA)
            nc.vector.tensor_tensor(gam_qk[:], gam_q[:], gam_k[:], ALU.mult).then_inc(gamma_done, 1)
            normalize1(0, True)
            dve.wait_ge(w_hi_done, 1)
            nc.vector.tensor_tensor(gate_lo[:], gate_stage[:], gate_hi[:], ALU.subtract)
            split_lo(w_lo[:], w_stage[:], w_hi[:])
            ln_high(0, True)
            k_norms(0, 0, True)
            k_norms(0, 1, True)
            dve.wait_ge(gamma_done, 1)
            steps(dve, step)
            f = B - 1
            hidden_high(f, 0, False)
            route(f, *range(1, 10))
            hidden_high(f, 1, False)
            route(f, *range(10, 19))
            hidden_high(f, 2, False)
            add_shared(f, False)
            hidden_high(f, 3, False)
            add_expert(f, 0)
            add_expert(f, 1)
            hidden_high(f, 4, False)
            add_expert(f, 2)
            add_expert(f, 3)
            hidden_high(f, 5, False)
            for e in range(4, E):
                add_expert(f, e)

        @block.gpsimd
        def _(pool):
            def inverse_root(dst, src, done):
                nc.gpsimd.tensor_tensor(dst, src, minus_half[0:src.shape[0], 0:src.shape[1]], ALU.pow).then_inc(done, 1)

            def rstd_first(b, first):
                pool.wait_ge(var1_done, b + 1)
                if not first:
                    pool.wait_ge(x_hat_done, b)
                inverse_root(rstd1[:], var1[:], rstd1_done)

            def ln_low(b):
                pool.wait_ge(ln_hi_done, b + 1)
                nc.gpsimd.tensor_tensor(ln_lo[:], ln_t[:], ln_hi[:], ALU.subtract).then_inc(ln_lo_done, 1)

            def residual(b, first):
                pool.wait_ge(x_loaded, b * DMA + DMA)
                if not first:
                    pool.wait_ge(x1_done, b)
                nc.gpsimd.tensor_tensor(x_res[:], x_in[:], bout_row[:].unsqueeze(1).to_broadcast([P, T, D]),
                                        ALU.add).then_inc(x_res_done, 1)

            def q_scales(b, first):
                pool.wait_ge(q_norm_done, b + 1)
                if not first:
                    pool.wait_ge(prob_done, b * U)
                inverse_root(q_scale[:], q_norm[:], q_scale_done)

            def k_scales(b, part, first):
                cols = slice(PARTS[part].start * H, PARTS[part].stop * H)
                pool.wait_ge(k_norm_done, b * 2 + part + 1)
                if not first:
                    pool.wait_ge(k_rms_done, b * CH)
                inverse_root(k_scale[:, cols], k_norm[:, cols], k_scale_done)

            def rstd_second(b, first):
                pool.wait_ge(var2_done, b + 1)
                if not first:
                    pool.wait_ge(x2_hat_done, b)
                inverse_root(rstd2[:], var2[:], rstd2_done)

            def hidden_low(b, p):
                pool.wait_ge(hid_hi_done, b * PAIRS + p + 1)
                nc.gpsimd.tensor_tensor(hid_lo[:, p % HID_RING, :], relu2[:, p % 2, :], hid_hi[:, p % HID_RING, :],
                                        ALU.subtract).then_inc(hid_lo_done, 1)

            def step(b, experts, following):
                first = isinstance(b, int) and b == 0

                def low(p):
                    if experts:
                        hidden_low(b - 1, p)

                low(0)
                q_scales(b, first)
                for p in range(1, 4):
                    low(p)
                if following:
                    rstd_first(b + 1, False)
                low(4)
                low(5)
                if following:
                    ln_low(b + 1)
                rstd_second(b, first)
                if following:
                    k_scales(b + 1, 0, False)
                    k_scales(b + 1, 1, False)
                    residual(b + 1, False)

            for dst, src in ((ln_g[:, 0, :], g_l), (ln_g[:, 1, :], g_x), (ln_b[:, 0, :], b_l), (ln_b[:, 1, :], b_x)):
                pool.dma_start(dst, src).then_inc(vectors_in, DMA)
            for h in range(2):
                rows = slice(h * DH, (h + 1) * DH)
                pool.dma_start(gam_q[rows, :], q_gamma.rearrange("(d a) -> d a", a=1)).then_inc(vectors_in, DMA)
                pool.dma_start(gam_k[rows, :], k_gamma.rearrange("(d a) -> d a", a=1)).then_inc(vectors_in, DMA)
            pool.dma_start(bout_row[:], b_out.partition_broadcast(P)).then_inc(vectors_in, DMA)
            pool.dma_start(gbias[:], gate_bias.partition_broadcast(P)).then_inc(vectors_in, DMA)
            nc.gpsimd.memset(minus_half[:], -0.5)
            nc.gpsimd.memset(mask_row[:, 0:S], 0.0)
            nc.gpsimd.memset(k_hi[:, :, KEYS:KPAD].bitcast(F32), 0.0)
            nc.gpsimd.memset(k_lo[:, :, KEYS:KPAD].bitcast(F32), 0.0)
            nc.gpsimd.memset(var1[:], 1.0).then_inc(zeroed, 1)
            nc.gpsimd.memset(ident[:], 0.0)
            nc.gpsimd.memset(lower[:], 0.0).then_inc(zeroed, 1)
            pool.wait_ge(zeroed, 2)
            for e in range(1, E):
                nc.gpsimd.memset(lower[:, e, 0:e], 1.0)
            nc.gpsimd.affine_select(out=ident[:], in_=ident[:], compare_op=ALU.not_equal, fill=1.0, base=0,
                                    pattern=[[-1, P]], channel_multiplier=1).then_inc(consts, 1)
            rstd_first(0, True)
            pool.wait_ge(vectors_in, 10 * DMA)
            residual(0, True)
            ln_low(0)
            k_scales(0, 0, True)
            k_scales(0, 1, True)
            steps(pool, step)
            for p in range(PAIRS):
                hidden_low(B - 1, p)


_INS = ["x", "ctx", "mask", "g_x", "b_x", "g_l", "b_l", "q_gamma", "k_gamma", "w_q", "w_kv", "w_out", "b_out",
        "gate_t", "gate_bias", "up_t", "down_t"]


def kernel(x, ctx_1024, mask_BxS2_bk0, L0_xattn_ln_x_g, L0_xattn_ln_x_b, L0_xattn_ln_l_g, L0_xattn_ln_l_b,
           L0_xattn_q_gamma, L0_xattn_k_gamma, L0_xattn_W_q, L0_xattn_W_kv, L0_xattn_W_out, L0_xattn_b_out,
           L0_ffn_gate_weight, L0_ffn_gate_bias, L0_ffn_up_weights, L0_ffn_down_weights,
           L0_ffn_shared_up_weight, L0_ffn_shared_down_weight):
    import numpy as np
    import concourse.bacc as bacc
    from concourse.bass_utils import run_bass_kernel_spmd

    x = np.ascontiguousarray(x)
    up, down = np.asarray(L0_ffn_up_weights), np.asarray(L0_ffn_down_weights)
    experts, inner, dim = up.shape
    up_t = np.concatenate([np.asarray(L0_ffn_shared_up_weight), up.reshape(experts * inner, dim)], axis=0).T
    down_t = np.concatenate([np.asarray(L0_ffn_shared_down_weight).T,
                             down.transpose(0, 2, 1).reshape(experts * inner, dim)], axis=0)
    columns = [np.asarray(v).reshape(-1, 128).T for v in (L0_xattn_ln_x_g, L0_xattn_ln_x_b,
                                                         L0_xattn_ln_l_g, L0_xattn_ln_l_b)]
    given = [x, ctx_1024, mask_BxS2_bk0, *columns, L0_xattn_q_gamma, L0_xattn_k_gamma, L0_xattn_W_q, L0_xattn_W_kv,
             L0_xattn_W_out, L0_xattn_b_out, np.asarray(L0_ffn_gate_weight).T, L0_ffn_gate_bias, up_t, down_t]

    nc = bacc.Bacc("TRN2", target_bir_lowering=False, num_devices=1)
    arrays, args = {}, []
    for name, a in zip(_INS, given):
        a = np.ascontiguousarray(a)
        arrays[f"in_{name}"] = a
        args.append(nc.dram_tensor(f"in_{name}", a.shape, mybir.dt.from_np(a.dtype), kind="ExternalInput").ap())
    out = nc.dram_tensor("out", x.shape, mybir.dt.float32, kind="ExternalOutput").ap()
    build(nc, *args, out)
    r = run_bass_kernel_spmd(nc, [arrays], core_ids=[0])
    return r.results[0]["out"]
```

```python
from contextlib import ExitStack

import concourse.bass as bass
from concourse import mybir

F32 = mybir.dt.float32
F32R = mybir.dt.float32r
U8 = mybir.dt.uint8
ALU = mybir.AluOpType
ACT = mybir.ActivationFunctionType
AX_X = mybir.AxisListType.X

LN_EPS = 1e-5
RMS_EPS = 1e-8
MASKED = 3.0e38
ROUTED_SCALE = 2.5
DMA = 16


def build(nc, x, ctx_in, mask, g_x, b_x, g_l, b_l, q_gamma, k_gamma, w_q, w_kv, w_out, b_out,
          gate_t, gate_bias, up_t, down_t, out):
    B, S, D = x.shape
    C = ctx_in.shape[1]
    P = 128
    DH = q_gamma.shape[0]
    H = D // DH
    T = S // P
    FT = D // P
    KEYS = S + C
    CH = 3
    KC = KEYS // CH
    KPAD = KEYS + KEYS % 2
    E = gate_t.shape[1]
    F = up_t.shape[1] // P
    FS = F - E
    PAIRS = F // 2
    SP_PAIRS = FS // 2
    U = T * H
    G = E // 4
    assert KC * CH == KEYS and KC <= P and D == 256 and S == 256 and 2 * DH == P and FS == 4
    ACC = 1 + 2 * E

    with ExitStack() as stack:
        def sb(name, shape, dt=F32):
            return stack.enter_context(nc.sbuf_tensor(name, shape, dt))

        def sem(name):
            return stack.enter_context(nc.semaphore(name))

        ident = sb("ident", [P, P])
        head_sel = sb("head_sel", [P, 2])
        lower = sb("lower", [P, E, E])
        minus_half = sb("minus_half", [P, 16])
        ln_g = sb("ln_g", [P, 2, FT])
        ln_b = sb("ln_b", [P, 2, FT])
        gam_q = sb("gam_q", [P, 1])
        gam_k = sb("gam_k", [P, 1])
        gam_qk = sb("gam_qk", [P, 1])
        bout_row = sb("bout_row", [P, D])
        gbias = sb("gbias", [P, E])
        w_stage = sb("w_stage", [P, FT, 4 * D])
        up_stage = sb("up_stage", [P, FT, F * P])
        down_stage = sb("down_stage", [P, F, D])
        gate_stage = sb("gate_stage", [P, FT, E])
        w_hi, w_lo = sb("w_hi", [P, FT, 4 * D], F32R), sb("w_lo", [P, FT, 4 * D], F32R)
        up_hi, up_lo = sb("up_hi", [P, FT, F * P], F32R), sb("up_lo", [P, FT, F * P], F32R)
        down_hi, down_lo = sb("down_hi", [P, F, D], F32R), sb("down_lo", [P, F, D], F32R)
        gate_parts = sb("gate_parts", [P, FT, 2 * E], F32R)

        x_in = sb("x_in", [P, T, D])
        c_in = sb("c_in", [C, D])
        mask_in = sb("mask_in", [P, C], U8)
        mask_row = sb("mask_row", [P, KEYS])
        x_res = sb("x_res", [P, T, D])
        stats1 = sb("stats1", [P, T + 1, 6])
        mv1 = sb("mv1", [P, T + 1, 2])
        var1 = sb("var1", [P, T + 1])
        rstd1 = sb("rstd1", [P, T + 1])
        x_hat = sb("x_hat", [P, T, D])
        c_hat = sb("c_hat", [C, D])
        ln_t = sb("ln_t", [P, FT, KEYS])
        ln_hi, ln_lo = sb("ln_hi", [P, FT, KEYS], F32R), sb("ln_lo", [P, FT, KEYS], F32R)
        q_hi, q_lo = sb("q_hi", [P, FT, S], F32R), sb("q_lo", [P, FT, S], F32R)
        q_sq = sb("q_sq", [P, FT, S])
        q_norm = sb("q_norm", [P, U])
        q_scale = sb("q_scale", [P, U])
        k_sq = sb("k_sq", [KC, CH, D])
        k_sum = sb("k_sum", [KC, CH * H])
        k_norm = sb("k_norm", [KC, CH * H])
        k_scale = sb("k_scale", [KC, CH * H])
        k_rms = sb("k_rms", [KC, CH, D])
        v_sb = sb("v_sb", [KC, CH, D])
        k_hi, k_lo = sb("k_hi", [P, FT, KPAD], F32R), sb("k_lo", [P, FT, KPAD], F32R)

        masked = sb("masked", [P, U, KEYS])
        row_max = sb("row_max", [P, U])
        neg_max = sb("neg_max", [P, U])
        probs = sb("probs", [P, U, KEYS])
        row_sum = sb("row_sum", [P, U])
        row_inv = sb("row_inv", [P, U])
        PT_RING = 3
        probs_t = sb("probs_t", [KC, PT_RING, CH * P])
        attn = sb("attn", [P, U, DH])
        at_hi, at_lo = sb("at_hi", [P, FT, S], F32R), sb("at_lo", [P, FT, S], F32R)
        x1 = sb("x1", [P, T, D])
        stats2 = sb("stats2", [P, T, 6])
        mv2 = sb("mv2", [P, T, 2])
        var2 = sb("var2", [P, T])
        rstd2 = sb("rstd2", [P, T])
        x2_hat = sb("x2_hat", [P, T, D])
        x2_hi, x2_lo = sb("x2_hi", [P, FT, S], F32R), sb("x2_lo", [P, FT, S], F32R)

        logits = sb("logits", [P, T, E])
        exp_neg = sb("exp_neg", [P, T, E])
        sig_den = sb("sig_den", [P, T, E])
        score = sb("score", [P, T, E])
        biased = sb("biased", [P, T, E])
        pair_hi = sb("pair_hi", [P, T * G, 2])
        pair_lo = sb("pair_lo", [P, T * G, 2])
        top1 = sb("top1", [P, T * G])
        mid_a = sb("mid_a", [P, T * G])
        mid_b = sb("mid_b", [P, T * G])
        top2 = sb("top2", [P, T * G])
        group_sum = sb("group_sum", [P, T, G])
        group_sel = sb("group_sel", [P, T, G])
        in_group = sb("in_group", [P, T, E])
        above = sb("above", [P, T, E, E])
        tied = sb("tied", [P, T, E, E])
        tied_low = sb("tied_low", [P, T, E, E])
        beats = sb("beats", [P, T, E, E])
        rank = sb("rank", [P, T, E])
        picked = sb("picked", [P, T, E])
        pick_sum = sb("pick_sum", [P, T])
        pick_eps = sb("pick_eps", [P, T])
        pick_inv = sb("pick_inv", [P, T])
        route_w = sb("route_w", [P, T, E])
        relu_sb = sb("relu_sb", [P, 2, 2 * S])
        relu2 = sb("relu2", [P, 2, 2 * S])
        HID_RING = 3
        hid_hi = sb("hid_hi", [P, HID_RING, 2 * S], F32R)
        hid_lo = sb("hid_lo", [P, HID_RING, 2 * S], F32R)
        acc = sb("acc", [P, T, D])
        carrier = sb("carrier", [P, 1])

        attn_ps = stack.enter_context(nc.psum_tensor("attn_ps", [P, 4, 512], F32))
        up_ps = stack.enter_context(nc.psum_tensor("up_ps", [P, 2, 512], F32))
        down_ps = stack.enter_context(nc.psum_tensor("down_ps", [P, 2, 512], F32))

        weights_in, up_in, down_in = sem("weights_in"), sem("up_in"), sem("down_in")
        vectors_in = sem("vectors_in")
        x_loaded, c_loaded, mask_loaded = sem("x_loaded"), sem("c_loaded"), sem("mask_loaded")
        stored = sem("stored")
        consts, zeroed = sem("consts"), sem("zeroed")
        w_hi_done, w_lo_done = sem("w_hi_done"), sem("w_lo_done")
        gamma_done, head_sel_done = sem("gamma_done"), sem("head_sel_done")
        lnt_ps, q_ps, kv_ps, qn_ps, kt_ps = sem("lnt_ps"), sem("q_ps"), sem("kv_ps"), sem("qn_ps"), sem("kt_ps")
        score_ps, pt_ps, pv_ps = sem("score_ps"), sem("pt_ps"), sem("pv_ps")
        at_ps, out_ps, x2t_ps, logit_ps = sem("at_ps"), sem("out_ps"), sem("x2t_ps"), sem("logit_ps")
        up_done, down_done = sem("up_done"), sem("down_done")
        ln_full_done = sem("ln_full_done")
        q_hi_done, q_sq_done = sem("q_hi_done"), sem("q_sq_done")
        k_sq_done, v_done, k_hi_done = sem("k_sq_done"), sem("v_done"), sem("k_hi_done")
        prob_done, pt_done = sem("prob_done"), sem("pt_done")
        at_hi_done, x2_hi_done, exp_neg_done = sem("at_hi_done"), sem("x2_hi_done"), sem("exp_neg_done")
        relu_done, relu2_done = sem("relu_done"), sem("relu2_done")
        ln1_step, var1_done, x_hat_done, mask_done = sem("ln1_step"), sem("var1_done"), sem("x_hat_done"), sem("mask_done")
        ln_hi_done, q_lo_done, q_norm_done = sem("ln_hi_done"), sem("q_lo_done"), sem("q_norm_done")
        k_sum_done, k_norm_done, k_rms_done, k_lo_done = sem("k_sum_done"), sem("k_norm_done"), sem("k_rms_done"), sem("k_lo_done")
        masked_done, neg_max_done = sem("masked_done"), sem("neg_max_done")
        row_inv_done, attn_done, at_lo_done, x1_done = sem("row_inv_done"), sem("attn_done"), sem("at_lo_done"), sem("x1_done")
        ln2_step, var2_done, x2_hat_done, x2_lo_done = sem("ln2_step"), sem("var2_done"), sem("x2_hat_done"), sem("x2_lo_done")
        logits_done, router_step = sem("logits_done"), sem("router_step")
        hid_hi_done, acc_done = sem("hid_hi_done"), sem("acc_done")
        rstd1_done, ln_lo_done, x_res_done = sem("rstd1_done"), sem("ln_lo_done"), sem("x_res_done")
        q_scale_done, k_scale_done, rstd2_done, hid_lo_done = sem("q_scale_done"), sem("k_scale_done"), sem("rstd2_done"), sem("hid_lo_done")

        PARTS = (slice(1, 3), slice(0, 1))
        LN1_STEPS = 2 * (T + 1)
        LN2_STEPS = 2 * T
        ROUTER_STEPS = 23

        block = stack.enter_context(nc.Block())

        def steps(eng, step):
            step(0, False, True)
            step(1, True, True)
            with eng.Fori(2, B - 1) as b:
                step(b, True, True)
            step(B - 1, True, False)

        @block.sync
        def _(sp):
            def load(b, first):
                if not first:
                    sp.wait_ge(x_hat_done, b)
                    sp.wait_ge(x_res_done, b)
                    sp.wait_ge(mask_done, b)
                sp.dma_start(x_in[:], x[b].rearrange("(t p) d -> p t d", p=P)).then_inc(x_loaded, DMA)
                sp.dma_start(c_in[:], ctx_in[b]).then_inc(c_loaded, DMA)
                sp.dma_start(mask_in[:], mask[b].partition_broadcast(P)).then_inc(mask_loaded, DMA)

            def store(b):
                sp.wait_ge(acc_done, b * ACC + ACC)
                sp.dma_start(out[b].rearrange("(t p) d -> p t d", p=P), acc[:]).then_inc(stored, DMA)

            load(0, True)
            sp.dma_start(w_stage[:, :, 0:D], w_q.rearrange("(k p) n -> p k n", p=P)).then_inc(weights_in, DMA)
            sp.dma_start(w_stage[:, :, D:3 * D], w_kv.rearrange("(k p) n -> p k n", p=P)).then_inc(weights_in, DMA)
            sp.dma_start(w_stage[:, :, 3 * D:4 * D], w_out.rearrange("(k p) n -> p k n", p=P)).then_inc(weights_in, DMA)
            sp.dma_start(gate_stage[:], gate_t.rearrange("(k p) n -> p k n", p=P)).then_inc(weights_in, DMA)
            sp.dma_start(up_stage[:], up_t.rearrange("(k p) n -> p k n", p=P)).then_inc(up_in, DMA)
            sp.dma_start(down_stage[:], down_t.rearrange("(f p) n -> p f n", p=P)).then_inc(down_in, DMA)
            load(1, False)

            def step(b, experts, following):
                if following and not (isinstance(b, int) and b == 0):
                    load(b + 1, False)
                if experts:
                    store(b - 1)

            steps(sp, step)
            store(B - 1)
            sp.wait_ge(stored, B * DMA)

        @block.tensor
        def _(pe):
            def split_product(out_ap, stationary, moving, first, last):
                (s_hi, s_lo), (m_hi, m_lo) = stationary, moving
                nc.tensor.matmul(out_ap, s_hi, m_hi, start=first, stop=False)
                nc.tensor.matmul(out_ap, s_hi, m_lo, start=False, stop=False)
                return nc.tensor.matmul(out_ap, s_lo, m_hi, start=False, stop=last)

            def transpose_ln(b, experts):
                pe.wait_ge(x_hat_done, b + 1)
                if not (isinstance(b, int) and b == 0) and not experts:
                    pe.wait_ge(q_lo_done, b)
                for ft in range(FT):
                    if experts:
                        pe.wait_ge(relu_done, (b - 2) * PAIRS + PAIRS - 1 + ft)
                    for t in range(T):
                        nc.tensor.transpose(up_ps[:, ft, t * P:(t + 1) * P], x_hat[:, t, ft * P:(ft + 1) * P], ident[:])
                    nc.tensor.transpose(up_ps[:, ft, S:KEYS], c_hat[:, ft * P:(ft + 1) * P],
                                        ident[0:C, 0:C]).then_inc(lnt_ps, 1)

            def project_q(b):
                for ft in range(FT):
                    for k in range(FT):
                        cols = slice(ft * P, (ft + 1) * P)
                        last = split_product(up_ps[:, 0, ft * S:(ft + 1) * S],
                                             (w_hi[:, k, cols], w_lo[:, k, cols]),
                                             (ln_hi[:, k, 0:S], ln_lo[:, k, 0:S]), k == 0, k == FT - 1)
                last.then_inc(q_ps, 1)

            def project_kv(b, c):
                if c == 1:
                    pe.wait_ge(ln_hi_done, (b + 1) * FT)
                    pe.wait_ge(ln_lo_done, (b + 1) * FT)
                if not (isinstance(b, int) and b == 0):
                    pe.wait_ge(pt_done, b * U - {1: 2, 2: 1, 0: 0}[c])
                rows = slice(c * KC, (c + 1) * KC)
                for k in range(FT):
                    last = split_product(attn_ps[0:KC, c, :], (ln_hi[:, k, rows], ln_lo[:, k, rows]),
                                         (w_hi[:, k, D:3 * D], w_lo[:, k, D:3 * D]), k == 0, k == FT - 1)
                last.then_inc(kv_ps, 1)

            def sum_q_squares(b, first):
                pe.wait_ge(q_sq_done, b + 1)
                if first:
                    pe.wait_ge(head_sel_done, 1)
                for t in range(T):
                    for ft in range(FT):
                        last = nc.tensor.matmul(attn_ps[:, 0, t * H + 2 * ft:t * H + 2 * ft + 2],
                                                q_sq[:, ft, t * P:(t + 1) * P], head_sel[:], start=True, stop=True)
                last.then_inc(qn_ps, 1)

            def transpose_k(b):
                for part in range(2):
                    pe.wait_ge(k_rms_done, b * 2 + part + 1)
                    if part == 0:
                        pe.wait_ge(v_done, b * 2 + 1)
                    for ft in range(FT):
                        for c in range(PARTS[part].start, PARTS[part].stop):
                            last = nc.tensor.transpose(attn_ps[:, 1 + ft, c * KC:(c + 1) * KC],
                                                       k_rms[:, c, ft * P:(ft + 1) * P], ident[0:KC, 0:KC])
                        if part == 1:
                            last.then_inc(kt_ps, 1)

            def scores(b, u):
                t, h = divmod(u, H)
                if u == 0:
                    pe.wait_ge(q_norm_done, b + 1)
                if u < 2:
                    pe.wait_ge(k_hi_done, b * FT + u + 1)
                    pe.wait_ge(k_lo_done, b * FT + u + 1)
                elif u >= 3:
                    pe.wait_ge(masked_done, b * U + u - 2)
                ft, rows = h // 2, slice((h % 2) * DH, (h % 2 + 1) * DH)
                cols = slice(t * P, (t + 1) * P)
                split_product(attn_ps[:, u % 3, 0:KPAD], (q_hi[rows, ft, cols], q_lo[rows, ft, cols]),
                              (k_hi[rows, ft, :], k_lo[rows, ft, :]), True, True).then_inc(score_ps, 1)

            def transpose_probs(b, u):
                pe.wait_ge(prob_done, b * U + u + 1)
                if u < 3:
                    pe.wait_ge(masked_done, b * U + 6 + u)
                else:
                    pe.wait_ge(pt_done, b * U + u - 2)
                for c in range(CH):
                    last = nc.tensor.transpose(attn_ps[0:KC, (u + 2) % 3, c * P:(c + 1) * P],
                                               probs[:, u, c * KC:(c + 1) * KC], ident[:])
                last.then_inc(pt_ps, 1)

            def probs_times_v(b, u, first):
                if u == 0:
                    if not first:
                        pe.wait_ge(x2_lo_done, b * FT)
                        pe.wait_ge(logits_done, b)
                    pe.wait_ge(v_done, b * 2 + 2)
                pe.wait_ge(pt_done, b * U + u + 1)
                h = u % H
                for c in range(CH):
                    last = nc.tensor.matmul(attn_ps[:, 3, u * DH:(u + 1) * DH],
                                            probs_t[:, u % PT_RING, c * P:(c + 1) * P],
                                            v_sb[:, c, h * DH:(h + 1) * DH], start=(c == 0), stop=(c == CH - 1))
                last.then_inc(pv_ps, 1)

            def transpose_attn(b, following):
                pe.wait_ge(attn_done, b + 1)
                if following:
                    pe.wait_ge(ln_full_done, (b + 2) * FT)
                else:
                    pe.wait_ge(relu_done, b * PAIRS)
                for ft in range(FT):
                    for t in range(T):
                        last = nc.tensor.transpose(up_ps[:, ft, t * P:(t + 1) * P],
                                                   attn[:, t * H + 2 * ft:t * H + 2 * ft + 2, :], ident[:])
                    last.then_inc(at_ps, 1)

            def project_out(b):
                pe.wait_ge(at_hi_done, (b + 1) * FT)
                pe.wait_ge(at_lo_done, (b + 1) * FT)
                for t in range(T):
                    for k in range(FT):
                        cols = slice(t * P, (t + 1) * P)
                        last = split_product(attn_ps[:, 3, t * D:(t + 1) * D], (at_hi[:, k, cols], at_lo[:, k, cols]),
                                             (w_hi[:, k, 3 * D:4 * D], w_lo[:, k, 3 * D:4 * D]), k == 0, k == FT - 1)
                last.then_inc(out_ps, 1)

            def transpose_x2(b):
                pe.wait_ge(x2_hat_done, b + 1)
                for ft, bank in enumerate((attn_ps[:, 3, 0:S], up_ps[:, 1, 0:S])):
                    for t in range(T):
                        last = nc.tensor.transpose(bank[:, t * P:(t + 1) * P], x2_hat[:, t, ft * P:(ft + 1) * P],
                                                   ident[:])
                    last.then_inc(x2t_ps, 1)

            def router(b):
                pe.wait_ge(x2_hi_done, (b + 1) * FT)
                pe.wait_ge(x2_lo_done, (b + 1) * FT)
                for t in range(T):
                    for k in range(FT):
                        rows = slice(t * P, (t + 1) * P)
                        nc.tensor.matmul(attn_ps[:, 3, 2 * t * E:2 * (t + 1) * E], x2_hi[:, k, rows],
                                         gate_parts[:, k, :], start=k == 0, stop=False)
                        last = nc.tensor.matmul(attn_ps[:, 3, 2 * t * E:(2 * t + 1) * E], x2_lo[:, k, rows],
                                                gate_parts[:, k, 0:E], start=False, stop=k == FT - 1)
                last.then_inc(logit_ps, 1)

            def up(b, p, first, following=True):
                if first and p == 0:
                    pe.wait_ge(w_lo_done, 3)
                if p == 0:
                    pe.wait_ge(x2_hi_done, (b + 1) * FT)
                    pe.wait_ge(x2_lo_done, (b + 1) * FT)
                    if following:
                        pe.wait_ge(q_lo_done, b + 2)
                if p >= 2 or not first:
                    pe.wait_ge(relu_done, b * PAIRS + p - 1)
                for j in range(2):
                    for k in range(FT):
                        cols = slice((2 * p + j) * P, (2 * p + j + 1) * P)
                        last = split_product(up_ps[:, p % 2, j * S:(j + 1) * S], (up_hi[:, k, cols], up_lo[:, k, cols]),
                                             (x2_hi[:, k, :], x2_lo[:, k, :]), k == 0, k == FT - 1)
                last.then_inc(up_done, 1)

            def hidden(f, t):
                cols = slice((f % 2) * S + t * P, (f % 2) * S + (t + 1) * P)
                slot = (f // 2) % HID_RING
                return hid_hi[:, slot, cols], hid_lo[:, slot, cols]

            def down_shared(b, t, first):
                if t == 0:
                    pe.wait_ge(hid_hi_done, b * PAIRS + SP_PAIRS)
                    pe.wait_ge(hid_lo_done, b * PAIRS + SP_PAIRS)
                    if not first:
                        pe.wait_ge(acc_done, b * ACC)
                for f in range(FS):
                    last = split_product(down_ps[:, 0, t * D:(t + 1) * D], hidden(f, t),
                                         (down_hi[:, f, :], down_lo[:, f, :]), f == 0, f == FS - 1)
                if t == T - 1:
                    last.then_inc(down_done, 1)

            def down_expert(b, e, first):
                f = FS + e
                pe.wait_ge(hid_hi_done, b * PAIRS + f // 2 + 1)
                pe.wait_ge(hid_lo_done, b * PAIRS + f // 2 + 1)
                if e > 0:
                    pe.wait_ge(acc_done, b * ACC + 2 * e - 1)
                elif not first:
                    pe.wait_ge(acc_done, b * ACC - 2)
                for t in range(T):
                    last = split_product(down_ps[:, (e + 1) % 2, t * D:(t + 1) * D], hidden(f, t),
                                         (down_hi[:, f, :], down_lo[:, f, :]), True, True)
                last.then_inc(down_done, 1)

            def step(b, experts, following):
                first = isinstance(b, int) and b == 0
                f, f_first = (b - 1, isinstance(b, int) and b == 1)

                def ffn(what, n):
                    if experts:
                        if what == "up":
                            up(f, n, f_first)
                        elif what == "shared":
                            down_shared(f, n, f_first)
                        else:
                            down_expert(f, n, f_first)

                transpose_k(b)
                sum_q_squares(b, first)
                ffn("up", 0)
                ffn("up", 1)
                if experts:
                    router(f)
                scores(b, 0)
                scores(b, 1)
                ffn("up", 2)
                scores(b, 2)
                scores(b, 3)
                ffn("shared", 0)
                scores(b, 4)
                scores(b, 5)
                ffn("shared", 1)
                scores(b, 6)
                scores(b, 7)
                transpose_probs(b, 0)
                ffn("up", 3)
                transpose_probs(b, 1)
                probs_times_v(b, 0, first)
                ffn("down", 0)
                transpose_probs(b, 2)
                probs_times_v(b, 1, first)
                ffn("up", 4)
                transpose_probs(b, 3)
                probs_times_v(b, 2, first)
                ffn("down", 1)
                transpose_probs(b, 4)
                probs_times_v(b, 3, first)
                ffn("down", 2)
                transpose_probs(b, 5)
                ffn("up", 5)
                probs_times_v(b, 4, first)
                ffn("down", 3)
                if following:
                    transpose_ln(b + 1, experts)
                probs_times_v(b, 5, first)
                transpose_probs(b, 6)
                ffn("down", 4)
                transpose_probs(b, 7)
                ffn("down", 5)
                probs_times_v(b, 6, first)
                probs_times_v(b, 7, first)
                if following:
                    project_kv(b + 1, 1)
                transpose_attn(b, following)
                if following:
                    project_kv(b + 1, 2)
                project_out(b)
                if following:
                    project_kv(b + 1, 0)
                    project_q(b + 1)
                ffn("down", 6)
                ffn("down", 7)
                transpose_x2(b)

            pe.wait_ge(consts, 1)
            transpose_ln(0, False)
            pe.wait_ge(w_lo_done, 1)
            project_kv(0, 1)
            project_kv(0, 2)
            project_kv(0, 0)
            project_q(0)
            steps(pe, step)
            up(B - 1, 0, False, False)
            router(B - 1)
            up(B - 1, 1, False, False)
            up(B - 1, 2, False)
            for t in range(T):
                down_shared(B - 1, t, False)
            up(B - 1, 3, False)
            down_expert(B - 1, 0, False)
            down_expert(B - 1, 1, False)
            up(B - 1, 4, False)
            down_expert(B - 1, 2, False)
            down_expert(B - 1, 3, False)
            up(B - 1, 5, False)
            for e in range(4, E):
                down_expert(B - 1, e, False)

        @block.scalar
        def _(act):
            def split_hi(n, dst, src):
                nc.scalar.activation(dst, src, ACT.Copy).then_inc(w_hi_done, 1)

            def ln_full(b, first):
                if not first:
                    act.wait_ge(ln_hi_done, b * FT)
                    act.wait_ge(ln_lo_done, b * FT)
                for ft in range(FT):
                    act.wait_ge(lnt_ps, b * FT + ft + 1)
                    for k, cols in enumerate((slice(0, S), slice(S, KEYS))):
                        last = nc.scalar.activation(ln_t[:, ft, cols], up_ps[:, ft, cols], ACT.Identity,
                                                    bias=ln_b[:, k, ft:ft + 1], scale=ln_g[:, k, ft:ft + 1])
                    last.then_inc(ln_full_done, 1)

            def q_out(b, first):
                act.wait_ge(q_ps, b + 1)
                if not first:
                    act.wait_ge(score_ps, b * U)
                    act.wait_ge(qn_ps, b)
                qv = up_ps[:, 0, :].rearrange("p (f s) -> p f s", f=FT)
                nc.scalar.activation(q_hi[:], qv, ACT.Copy).then_inc(q_hi_done, 1)
                nc.scalar.activation(q_sq[:], qv, ACT.Square).then_inc(q_sq_done, 1)

            def k_squares(b, part, first):
                act.wait_ge(kv_ps, b * CH + 2 + part)
                if not first:
                    act.wait_ge(k_sum_done, b * 2)
                nc.scalar.activation(k_sq[:, PARTS[part], :], attn_ps[0:KC, PARTS[part], 0:D],
                                     ACT.Square).then_inc(k_sq_done, 1)

            def v_out(b, part, first):
                if not first:
                    act.wait_ge(pv_ps, b * U)
                nc.scalar.activation(v_sb[:, PARTS[part], :], attn_ps[0:KC, PARTS[part], D:2 * D],
                                     ACT.Copy).then_inc(v_done, 1)

            def k_high(b, first):
                for ft in range(FT):
                    act.wait_ge(kt_ps, b * FT + ft + 1)
                    if not first:
                        act.wait_ge(score_ps, b * U)
                    nc.scalar.activation(k_hi[:, ft, 0:KEYS], attn_ps[:, 1 + ft, 0:KEYS], ACT.Copy,
                                         scale=gam_qk[:]).then_inc(k_hi_done, 1)

            def softmax(b, u, first):
                act.wait_ge(neg_max_done, b * T + u // H + 1)
                if not first:
                    act.wait_ge(pt_ps, b * U - U + u + 1)
                    act.wait_ge(row_inv_done, b)
                nc.scalar.activation(probs[:, u, :], masked[:, u, :], ACT.Exp, bias=neg_max[:, u:u + 1],
                                     scale=q_scale[:, u:u + 1], accum_out=row_sum[:, u:u + 1]).then_inc(prob_done, 1)

            def pt_out(b, u, first):
                act.wait_ge(pt_ps, b * U + u + 1)
                if not first or u >= PT_RING:
                    act.wait_ge(pv_ps, b * U + u + 1 - PT_RING)
                nc.scalar.activation(probs_t[:, u % PT_RING, :], attn_ps[0:KC, (u + 2) % 3, 0:CH * P],
                                     ACT.Copy).then_inc(pt_done, 1)

            def attn_high(b, first):
                if not first:
                    act.wait_ge(out_ps, b)
                for ft in range(FT):
                    act.wait_ge(at_ps, b * FT + ft + 1)
                    nc.scalar.activation(at_hi[:, ft, :], up_ps[:, ft, 0:S], ACT.Copy).then_inc(at_hi_done, 1)

            def x2_high(b, first):
                if not first:
                    act.wait_ge(up_done, b * PAIRS)
                for ft, bank in enumerate((attn_ps[:, 3, 0:S], up_ps[:, 1, 0:S])):
                    act.wait_ge(x2t_ps, b * FT + ft + 1)
                    nc.scalar.activation(x2_hi[:, ft, :], bank, ACT.Copy).then_inc(x2_hi_done, 1)

            def router_exp(b, first):
                act.wait_ge(logits_done, b + 1)
                if not first:
                    act.wait_ge(router_step, (b - 1) * ROUTER_STEPS + 1)
                nc.scalar.activation(exp_neg[:], logits[:], ACT.Exp, scale=-1.0).then_inc(exp_neg_done, 1)

            def hidden(b, p, first):
                act.wait_ge(up_done, b * PAIRS + p + 1)
                nc.scalar.activation(relu_sb[:, p % 2, :], up_ps[:, p % 2, :], ACT.Relu).then_inc(relu_done, 1)
                act.wait_ge(relu_done, b * PAIRS + p + 1)
                if not first or p >= 2:
                    act.wait_ge(hid_hi_done, b * PAIRS + p - 1)
                    act.wait_ge(hid_lo_done, b * PAIRS + p - 1)
                nc.scalar.activation(relu2[:, p % 2, :], relu_sb[:, p % 2, :], ACT.Square).then_inc(relu2_done, 1)

            def step(b, experts, following):
                first = isinstance(b, int) and b == 0
                f, f_first = b - 1, isinstance(b, int) and b == 1
                ffn = (lambda p: hidden(f, p, f_first)) if experts else (lambda p: None)
                if first:
                    act.wait_ge(up_in, DMA)
                    split_hi(1, up_hi[:], up_stage[:])
                k_high(b, first)
                ffn(0)
                if first:
                    act.wait_ge(down_in, DMA)
                    split_hi(2, down_hi[:], down_stage[:])
                ffn(1)
                if experts:
                    router_exp(f, f_first)
                ffn(2)
                for u in range(4):
                    softmax(b, u, first)
                pt_out(b, 0, first)
                ffn(3)
                pt_out(b, 1, first)
                softmax(b, 4, first)
                pt_out(b, 2, first)
                softmax(b, 5, first)
                ffn(4)
                pt_out(b, 3, first)
                softmax(b, 6, first)
                pt_out(b, 4, first)
                softmax(b, 7, first)
                pt_out(b, 5, first)
                ffn(5)
                if following:
                    ln_full(b + 1, False)
                pt_out(b, 6, first)
                pt_out(b, 7, first)
                attn_high(b, first)
                if following:
                    for part in range(2):
                        k_squares(b + 1, part, False)
                        v_out(b + 1, part, False)
                    q_out(b + 1, False)
                x2_high(b, first)

            act.wait_ge(weights_in, 4 * DMA)
            nc.scalar.activation(gate_parts[:, :, 0:E], gate_stage[:], ACT.Copy)
            split_hi(0, w_hi[:], w_stage[:])
            act.wait_ge(vectors_in, 10 * DMA)
            ln_full(0, True)
            for part in range(2):
                k_squares(0, part, True)
                v_out(0, part, True)
            q_out(0, True)
            steps(act, step)
            hidden(B - 1, 0, False)
            router_exp(B - 1, False)
            for p in range(1, PAIRS):
                hidden(B - 1, p, False)

        @block.vector
        def _(dve):
            def carry():
                nc.vector.memset(carrier[:], 0.0)

            def layer_norm1(b, first):
                k = b * LN1_STEPS
                dve.wait_ge(x_loaded, b * DMA + DMA)
                for t in range(T):
                    nc.vector.bn_stats(stats1[:, t, :], x_in[:, t, :]).then_inc(ln1_step, 1)
                dve.wait_ge(c_loaded, b * DMA + DMA)
                nc.vector.bn_stats(stats1[0:C, T, :], c_in[:]).then_inc(ln1_step, 1)
                dve.wait_ge(mask_loaded, b * DMA + DMA)
                if not first:
                    dve.wait_ge(mask_done, b)
                dve.wait_ge(ln1_step, k + T + 1)
                nc.vector.tensor_scalar(mask_row[:, S:KEYS], mask_in[:], -1.0, MASKED, ALU.add, ALU.mult).then_inc(mask_done, 1)
                if first:
                    dve.wait_ge(zeroed, 1)
                for t in range(T + 1):
                    rows = P if t < T else C
                    nc.vector.bn_aggr(mv1[0:rows, t, :], stats1[0:rows, t, :]).then_inc(ln1_step, 1)
                dve.wait_ge(ln1_step, k + LN1_STEPS)
                if not first:
                    dve.wait_ge(rstd1_done, b)
                nc.vector.tensor_scalar(var1[:, 0:T], mv1[:, 0:T, 1], 1.0 + LN_EPS, LN_EPS * LN_EPS, ALU.mult, ALU.add)
                nc.vector.tensor_scalar(var1[0:C, T:T + 1], mv1[0:C, T, 1:2], LN_EPS, None, ALU.add).then_inc(var1_done, 1)

            def normalize1(b, first):
                dve.wait_ge(rstd1_done, b + 1)
                if not first:
                    dve.wait_ge(lnt_ps, b * FT)
                for t in range(T):
                    nc.vector.tensor_scalar(x_hat[:, t, :], x_in[:, t, :], mv1[:, t, 0:1], rstd1[:, t:t + 1],
                                            ALU.subtract, ALU.mult)
                nc.vector.tensor_scalar(c_hat[:], c_in[:], mv1[0:C, T, 0:1], rstd1[0:C, T:T + 1],
                                        ALU.subtract, ALU.mult).then_inc(x_hat_done, 1)

            def ln_high(b, first):
                if not first:
                    dve.wait_ge(q_ps, b)
                for ft in range(FT):
                    dve.wait_ge(ln_full_done, b * FT + ft + 1)
                    nc.vector.tensor_copy(ln_hi[:, ft, :], ln_t[:, ft, :]).then_inc(ln_hi_done, 1)

            def q_low(b):
                dve.wait_ge(q_hi_done, b + 1)
                dve.wait_ge(q_sq_done, b + 1)
                nc.vector.tensor_tensor(q_lo[:], up_ps[:, 0, :].rearrange("p (f s) -> p f s", f=FT), q_hi[:],
                                        ALU.subtract).then_inc(q_lo_done, 1)

            def q_norms(b, first):
                dve.wait_ge(qn_ps, b + 1)
                if not first:
                    dve.wait_ge(q_scale_done, b)
                nc.vector.tensor_scalar(q_norm[:], attn_ps[:, 0, 0:U], DH * RMS_EPS * RMS_EPS, None,
                                        ALU.max).then_inc(q_norm_done, 1)

            def k_norms(b, part, first):
                cs = PARTS[part]
                cols = slice(cs.start * H, cs.stop * H)
                dve.wait_ge(k_sq_done, b * 2 + part + 1)
                nc.vector.tensor_reduce(k_sum[:, cols], k_sq[:, cs, :].rearrange("p c (h d) -> p (c h) d", d=DH), AX_X,
                                        ALU.add).then_inc(k_sum_done, 1)
                dve.wait_ge(k_sum_done, b * 2 + part + 1)
                if not first:
                    dve.wait_ge(k_scale_done, b * 2)
                nc.vector.tensor_scalar(k_norm[:, cols], k_sum[:, cols], 1.0 / DH, RMS_EPS * RMS_EPS, ALU.mult,
                                        ALU.max).then_inc(k_norm_done, 1)

            def k_normalize(b, part, first):
                cs = PARTS[part]
                n = cs.stop - cs.start
                dve.wait_ge(k_scale_done, b * 2 + part + 1)
                dve.wait_ge(v_done, b * 2 + part + 1)
                if not first:
                    dve.wait_ge(kt_ps, b * FT)
                nc.vector.tensor_tensor(
                    k_rms[:, cs, :].rearrange("p c (h d) -> p c h d", d=DH),
                    attn_ps[0:KC, cs, 0:D].rearrange("p c (h d) -> p c h d", d=DH),
                    k_scale[:, cs.start * H:cs.stop * H].rearrange("p (c h) -> p c h", c=n).unsqueeze(3)
                    .to_broadcast([KC, n, H, DH]), ALU.mult).then_inc(k_rms_done, 1)

            def k_low(b, ft):
                dve.wait_ge(k_hi_done, b * FT + ft + 1)
                nc.vector.scalar_tensor_tensor(k_lo[:, ft, 0:KEYS], attn_ps[:, 1 + ft, 0:KEYS], gam_qk[:],
                                               k_hi[:, ft, 0:KEYS], ALU.mult, ALU.subtract).then_inc(k_lo_done, 1)

            def mask_scores(b, u, first):
                if u % 2 == 0:
                    dve.wait_ge(score_ps, b * U + u + 2)
                    if not first:
                        dve.wait_ge(prob_done, b * U - U + u + 2)
                    if u == 0:
                        dve.wait_ge(mask_done, b + 1)
                    carry()
                nc.vector.tensor_tensor_reduce(masked[:, u, :], attn_ps[:, u % 3, 0:KEYS], mask_row[:], 1.0, -MASKED,
                                               ALU.add, ALU.max, row_max[:, u:u + 1]).then_inc(masked_done, 1)

            def negate_max(b, t):
                cols = slice(t * H, (t + 1) * H)
                dve.wait_ge(masked_done, b * U + (t + 1) * H)
                dve.wait_ge(q_scale_done, b + 1)
                nc.vector.scalar_tensor_tensor(neg_max[:, cols], row_max[:, cols], -1.0, q_scale[:, cols],
                                               ALU.mult, ALU.mult).then_inc(neg_max_done, 1)

            def invert_sums(b):
                dve.wait_ge(prob_done, b * U + U)
                nc.vector.reciprocal(row_inv[:], row_sum[:]).then_inc(row_inv_done, 1)

            def attn_out(b, first):
                dve.wait_ge(row_inv_done, b + 1)
                dve.wait_ge(pv_ps, b * U + U)
                if not first:
                    dve.wait_ge(at_ps, b * FT)
                nc.vector.tensor_tensor(attn[:], attn_ps[:, 3, :].rearrange("p (u d) -> p u d", d=DH),
                                        row_inv[:].unsqueeze(2).to_broadcast([P, U, DH]), ALU.mult).then_inc(attn_done, 1)

            def attn_low(b):
                for ft in range(FT):
                    dve.wait_ge(at_hi_done, b * FT + ft + 1)
                    nc.vector.tensor_tensor(at_lo[:, ft, :], up_ps[:, ft, 0:S], at_hi[:, ft, :],
                                            ALU.subtract).then_inc(at_lo_done, 1)

            def layer_norm2(b, first):
                k = b * LN2_STEPS
                dve.wait_ge(out_ps, b + 1)
                dve.wait_ge(x_res_done, b + 1)
                nc.vector.tensor_tensor(x1[:], attn_ps[:, 3, :].rearrange("p (t d) -> p t d", d=D), x_res[:],
                                        ALU.add).then_inc(x1_done, 1)
                dve.wait_ge(x1_done, b + 1)
                for t in range(T):
                    nc.vector.bn_stats(stats2[:, t, :], x1[:, t, :]).then_inc(ln2_step, 1)
                dve.wait_ge(ln2_step, k + T)
                carry()
                for t in range(T):
                    nc.vector.bn_aggr(mv2[:, t, :], stats2[:, t, :]).then_inc(ln2_step, 1)
                dve.wait_ge(ln2_step, k + LN2_STEPS)
                if not first:
                    dve.wait_ge(rstd2_done, b)
                nc.vector.tensor_scalar(var2[:], mv2[:, :, 1], LN_EPS, None, ALU.add).then_inc(var2_done, 1)

            def normalize2(b, first):
                dve.wait_ge(rstd2_done, b + 1)
                if not first:
                    dve.wait_ge(x2t_ps, b * FT)
                for t in range(T):
                    last = nc.vector.tensor_scalar(x2_hat[:, t, :], x1[:, t, :], mv2[:, t, 0:1], rstd2[:, t:t + 1],
                                                   ALU.subtract, ALU.mult)
                last.then_inc(x2_hat_done, 1)

            def x2_low(b):
                for ft, bank in enumerate((attn_ps[:, 3, 0:S], up_ps[:, 1, 0:S])):
                    dve.wait_ge(x2_hi_done, b * FT + ft + 1)
                    nc.vector.tensor_tensor(x2_lo[:, ft, :], bank, x2_hi[:, ft, :],
                                            ALU.subtract).then_inc(x2_lo_done, 1)

            def route(b, *levels):
                for level in levels:
                    route_level(b, level)

            def route_level(b, level):
                upto = (0, 1, 2, 3, 5, 8, 9, 10, 12, 13, 15, 16, 17, 18, 19, 20, 21, 22, 23)
                quad = biased[:].rearrange("p t (g a c) -> p (t g) a c", a=2, c=2)
                other = in_group[:].unsqueeze(2).to_broadcast([P, T, E, E])
                own = in_group[:].unsqueeze(3).to_broadcast([P, T, E, E])
                if level == 0:
                    dve.wait_ge(logit_ps, b + 1)
                elif level == 1:
                    dve.wait_ge(exp_neg_done, b + 1)
                else:
                    dve.wait_ge(router_step, b * ROUTER_STEPS + upto[level - 1])
                if level == 0:
                    nc.vector.tensor_reduce(logits[:], attn_ps[:, 3, 0:T * 2 * E].rearrange("p (t a e) -> p t e a", t=T, a=2),
                                            AX_X, ALU.add).then_inc(logits_done, 1)
                elif level == 1:
                    nc.vector.tensor_scalar(sig_den[:], exp_neg[:], 1.0, None, ALU.add).then_inc(router_step, 1)
                elif level == 2:
                    nc.vector.reciprocal(score[:], sig_den[:]).then_inc(router_step, 1)
                elif level == 3:
                    nc.vector.tensor_tensor(biased[:], score[:], gbias[:].unsqueeze(1).to_broadcast([P, T, E]),
                                            ALU.add).then_inc(router_step, 1)
                elif level == 4:
                    nc.vector.tensor_tensor(pair_hi[:], quad[:, :, :, 0], quad[:, :, :, 1], ALU.max).then_inc(router_step, 1)
                    nc.vector.tensor_tensor(pair_lo[:], quad[:, :, :, 0], quad[:, :, :, 1], ALU.min).then_inc(router_step, 1)
                elif level == 5:
                    nc.vector.tensor_tensor(top1[:], pair_hi[:, :, 0], pair_hi[:, :, 1], ALU.max).then_inc(router_step, 1)
                    nc.vector.tensor_tensor(mid_a[:], pair_hi[:, :, 0], pair_hi[:, :, 1], ALU.min).then_inc(router_step, 1)
                    nc.vector.tensor_tensor(mid_b[:], pair_lo[:, :, 0], pair_lo[:, :, 1], ALU.max).then_inc(router_step, 1)
                elif level == 6:
                    nc.vector.tensor_tensor(top2[:], mid_a[:], mid_b[:], ALU.max).then_inc(router_step, 1)
                elif level == 7:
                    nc.vector.tensor_tensor(group_sum[:].rearrange("p t g -> p (t g)"), top1[:], top2[:],
                                            ALU.add).then_inc(router_step, 1)
                elif level == 8:
                    nc.vector.tensor_tensor(group_sel[:, :, 0], group_sum[:, :, 0], group_sum[:, :, 1],
                                            ALU.is_ge).then_inc(router_step, 1)
                    nc.vector.tensor_tensor(group_sel[:, :, 1], group_sum[:, :, 0], group_sum[:, :, 1],
                                            ALU.is_lt).then_inc(router_step, 1)
                elif level == 9:
                    nc.vector.tensor_tensor(in_group[:].rearrange("p t (g q) -> p (t g) q", g=G),
                                            biased[:].rearrange("p t (g q) -> p (t g) q", g=G),
                                            group_sel[:].rearrange("p t g -> p (t g)").unsqueeze(2)
                                            .to_broadcast([P, T * G, E // G]), ALU.mult).then_inc(router_step, 1)
                elif level == 10:
                    nc.vector.tensor_tensor(above[:], other, own, ALU.is_gt).then_inc(router_step, 1)
                    nc.vector.tensor_tensor(tied[:], other, own, ALU.is_equal).then_inc(router_step, 1)
                elif level == 11:
                    nc.vector.tensor_tensor(tied_low[:], tied[:], lower[:].unsqueeze(1).to_broadcast([P, T, E, E]),
                                            ALU.mult).then_inc(router_step, 1)
                elif level == 12:
                    nc.vector.tensor_tensor(beats[:], above[:], tied_low[:], ALU.add).then_inc(router_step, 1)
                elif level == 13:
                    nc.vector.tensor_reduce(rank[:], beats[:], AX_X, ALU.add).then_inc(router_step, 1)
                elif level == 14:
                    nc.vector.scalar_tensor_tensor(picked[:], rank[:], 2.0, score[:], ALU.is_lt,
                                                   ALU.mult).then_inc(router_step, 1)
                elif level == 15:
                    nc.vector.tensor_reduce(pick_sum[:], picked[:], AX_X, ALU.add).then_inc(router_step, 1)
                elif level == 16:
                    nc.vector.tensor_scalar(pick_eps[:], pick_sum[:], 1e-20, None, ALU.add).then_inc(router_step, 1)
                elif level == 17:
                    nc.vector.reciprocal(pick_inv[:], pick_eps[:]).then_inc(router_step, 1)
                elif level == 18:
                    nc.vector.scalar_tensor_tensor(route_w[:], picked[:], ROUTED_SCALE,
                                                   pick_inv[:].unsqueeze(2).to_broadcast([P, T, E]),
                                                   ALU.mult, ALU.mult).then_inc(router_step, 1)

            def hidden_high(b, p, first):
                dve.wait_ge(relu2_done, b * PAIRS + p + 1)
                used = {0: -4, 1: -2, 2: 0, 3: 1, 4: 1, 5: 3}[p]
                if p >= HID_RING or not first:
                    dve.wait_ge(down_done, b * (E + 1) + used)
                nc.vector.tensor_copy(hid_hi[:, p % HID_RING, :], relu2[:, p % 2, :]).then_inc(hid_hi_done, 1)

            def add_shared(b, first):
                dve.wait_ge(down_done, b * (E + 1) + 1)
                if not first:
                    dve.wait_ge(stored, b * DMA)
                nc.vector.tensor_tensor(acc[:], down_ps[:, 0, :].rearrange("p (t d) -> p t d", d=D), x1[:],
                                        ALU.add).then_inc(acc_done, 1)

            def add_expert(b, e):
                dve.wait_ge(down_done, b * (E + 1) + e + 2)
                if e == 0:
                    dve.wait_ge(router_step, b * ROUTER_STEPS + ROUTER_STEPS)
                for t in range(T):
                    dve.wait_ge(acc_done, b * ACC + (2 * e + t if e else 1))
                    nc.vector.scalar_tensor_tensor(acc[:, t, :], down_ps[:, (e + 1) % 2, t * D:(t + 1) * D],
                                                   route_w[:, t, e:e + 1], acc[:, t, :], ALU.mult,
                                                   ALU.add).then_inc(acc_done, 1)

            def split_lo(dst, src, hi):
                nc.vector.tensor_tensor(dst, src, hi, ALU.subtract).then_inc(w_lo_done, 1)

            def step(b, experts, following):
                first = isinstance(b, int) and b == 0
                f, f_first = b - 1, isinstance(b, int) and b == 1

                def high(p):
                    if experts:
                        hidden_high(f, p, f_first)

                def add(e):
                    if experts:
                        add_expert(f, e)

                def routing(*levels):
                    if experts:
                        route(f, *levels)

                k_low(b, 0)
                k_low(b, 1)
                high(0)
                high(1)
                routing(0)
                if first:
                    dve.wait_ge(w_hi_done, 2)
                    split_lo(up_lo[:], up_stage[:], up_hi[:])
                    dve.wait_ge(w_hi_done, 3)
                    split_lo(down_lo[:], down_stage[:], down_hi[:])
                mask_scores(b, 0, first)
                mask_scores(b, 1, first)
                routing(1, 2, 3, 4, 5, 6)
                mask_scores(b, 2, first)
                mask_scores(b, 3, first)
                routing(7)
                negate_max(b, 0)
                routing(8)
                high(2)
                routing(9, 10)
                mask_scores(b, 4, first)
                mask_scores(b, 5, first)
                routing(11, 12)
                if experts:
                    add_shared(f, f_first)
                routing(13)
                mask_scores(b, 6, first)
                mask_scores(b, 7, first)
                routing(14)
                negate_max(b, 1)
                routing(15, 16)
                if following:
                    layer_norm1(b + 1, False)
                routing(17)
                high(3)
                routing(18)
                add(0)
                if following:
                    normalize1(b + 1, False)
                add(1)
                high(4)
                add(2)
                high(5)
                add(3)
                if following:
                    ln_high(b + 1, False)
                invert_sums(b)
                add(4)
                attn_out(b, first)
                add(5)
                attn_low(b)
                if following:
                    k_norms(b + 1, 0, False)
                layer_norm2(b, first)
                if following:
                    k_norms(b + 1, 1, False)
                normalize2(b, first)
                if following:
                    k_normalize(b + 1, 0, False)
                    k_normalize(b + 1, 1, False)
                    q_low(b + 1)
                x2_low(b)
                add(6)
                if following:
                    q_norms(b + 1, False)
                add(7)

            for h in range(2):
                for block_head in range(2):
                    last = nc.vector.memset(head_sel[h * DH:(h + 1) * DH, block_head:block_head + 1], float(h == block_head))
            last.then_inc(head_sel_done, 1)
            layer_norm1(0, True)
            dve.wait_ge(vectors_in, 10 * DMA)
            nc.vector.tensor_tensor(gam_qk[:], gam_q[:], gam_k[:], ALU.mult).then_inc(gamma_done, 1)
            normalize1(0, True)
            dve.wait_ge(w_hi_done, 1)
            nc.vector.tensor_tensor(gate_parts[:, :, E:2 * E], gate_stage[:], gate_parts[:, :, 0:E], ALU.subtract)
            split_lo(w_lo[:], w_stage[:], w_hi[:])
            ln_high(0, True)
            k_norms(0, 0, True)
            k_norms(0, 1, True)
            k_normalize(0, 0, True)
            k_normalize(0, 1, True)
            q_low(0)
            q_norms(0, True)
            dve.wait_ge(gamma_done, 1)
            steps(dve, step)
            f = B - 1
            hidden_high(f, 0, False)
            route(f, *range(10))
            hidden_high(f, 1, False)
            route(f, *range(10, 19))
            hidden_high(f, 2, False)
            add_shared(f, False)
            hidden_high(f, 3, False)
            add_expert(f, 0)
            add_expert(f, 1)
            hidden_high(f, 4, False)
            add_expert(f, 2)
            add_expert(f, 3)
            hidden_high(f, 5, False)
            for e in range(4, E):
                add_expert(f, e)

        @block.gpsimd
        def _(pool):
            def inverse_root(dst, src, done):
                nc.gpsimd.tensor_tensor(dst, src, minus_half[0:src.shape[0], 0:src.shape[1]], ALU.pow).then_inc(done, 1)

            def rstd_first(b, first):
                pool.wait_ge(var1_done, b + 1)
                if not first:
                    pool.wait_ge(x_hat_done, b)
                inverse_root(rstd1[:], var1[:], rstd1_done)

            def ln_low(b):
                for ft in range(FT):
                    pool.wait_ge(ln_hi_done, b * FT + ft + 1)
                    nc.gpsimd.tensor_tensor(ln_lo[:, ft, :], ln_t[:, ft, :], ln_hi[:, ft, :],
                                            ALU.subtract).then_inc(ln_lo_done, 1)

            def residual(b, first):
                pool.wait_ge(x_loaded, b * DMA + DMA)
                if not first:
                    pool.wait_ge(x1_done, b)
                nc.gpsimd.tensor_tensor(x_res[:], x_in[:], bout_row[:].unsqueeze(1).to_broadcast([P, T, D]),
                                        ALU.add).then_inc(x_res_done, 1)

            def q_scales(b, first):
                pool.wait_ge(q_norm_done, b + 1)
                if not first:
                    pool.wait_ge(prob_done, b * U)
                inverse_root(q_scale[:], q_norm[:], q_scale_done)

            def k_scales(b, part, first):
                cols = slice(PARTS[part].start * H, PARTS[part].stop * H)
                pool.wait_ge(k_norm_done, b * 2 + part + 1)
                if not first:
                    pool.wait_ge(k_rms_done, b * 2)
                inverse_root(k_scale[:, cols], k_norm[:, cols], k_scale_done)

            def rstd_second(b, first):
                pool.wait_ge(var2_done, b + 1)
                if not first:
                    pool.wait_ge(x2_hat_done, b)
                inverse_root(rstd2[:], var2[:], rstd2_done)

            def hidden_low(b, p):
                pool.wait_ge(hid_hi_done, b * PAIRS + p + 1)
                nc.gpsimd.tensor_tensor(hid_lo[:, p % HID_RING, :], relu2[:, p % 2, :], hid_hi[:, p % HID_RING, :],
                                        ALU.subtract).then_inc(hid_lo_done, 1)

            def step(b, experts, following):
                first = isinstance(b, int) and b == 0

                def low(p):
                    if experts:
                        hidden_low(b - 1, p)

                q_scales(b, first)
                for p in range(4):
                    low(p)
                if following:
                    rstd_first(b + 1, False)
                low(4)
                low(5)
                if following:
                    ln_low(b + 1)
                    k_scales(b + 1, 0, False)
                rstd_second(b, first)
                if following:
                    k_scales(b + 1, 1, False)
                    residual(b + 1, False)

            for dst, src in ((ln_g[:, 0, :], g_l), (ln_g[:, 1, :], g_x), (ln_b[:, 0, :], b_l), (ln_b[:, 1, :], b_x)):
                pool.dma_start(dst, src).then_inc(vectors_in, DMA)
            for h in range(2):
                rows = slice(h * DH, (h + 1) * DH)
                pool.dma_start(gam_q[rows, :], q_gamma.rearrange("(d a) -> d a", a=1)).then_inc(vectors_in, DMA)
                pool.dma_start(gam_k[rows, :], k_gamma.rearrange("(d a) -> d a", a=1)).then_inc(vectors_in, DMA)
            pool.dma_start(bout_row[:], b_out.partition_broadcast(P)).then_inc(vectors_in, DMA)
            pool.dma_start(gbias[:], gate_bias.partition_broadcast(P)).then_inc(vectors_in, DMA)
            nc.gpsimd.memset(minus_half[:], -0.5)
            nc.gpsimd.memset(mask_row[:, 0:S], 0.0)
            nc.gpsimd.memset(k_hi[:, :, KEYS:KPAD].bitcast(F32), 0.0)
            nc.gpsimd.memset(k_lo[:, :, KEYS:KPAD].bitcast(F32), 0.0)
            nc.gpsimd.memset(var1[:], 1.0).then_inc(zeroed, 1)
            nc.gpsimd.memset(ident[:], 0.0)
            nc.gpsimd.memset(lower[:], 0.0).then_inc(zeroed, 1)
            pool.wait_ge(zeroed, 2)
            for e in range(1, E):
                nc.gpsimd.memset(lower[:, e, 0:e], 1.0)
            nc.gpsimd.affine_select(out=ident[:], in_=ident[:], compare_op=ALU.not_equal, fill=1.0, base=0,
                                    pattern=[[-1, P]], channel_multiplier=1).then_inc(consts, 1)
            rstd_first(0, True)
            pool.wait_ge(vectors_in, 10 * DMA)
            residual(0, True)
            ln_low(0)
            k_scales(0, 0, True)
            k_scales(0, 1, True)
            steps(pool, step)
            for p in range(PAIRS):
                hidden_low(B - 1, p)


_INS = ["x", "ctx", "mask", "g_x", "b_x", "g_l", "b_l", "q_gamma", "k_gamma", "w_q", "w_kv", "w_out", "b_out",
        "gate_t", "gate_bias", "up_t", "down_t"]


def kernel(x, ctx_1024, mask_BxS2_bk0, L0_xattn_ln_x_g, L0_xattn_ln_x_b, L0_xattn_ln_l_g, L0_xattn_ln_l_b,
           L0_xattn_q_gamma, L0_xattn_k_gamma, L0_xattn_W_q, L0_xattn_W_kv, L0_xattn_W_out, L0_xattn_b_out,
           L0_ffn_gate_weight, L0_ffn_gate_bias, L0_ffn_up_weights, L0_ffn_down_weights,
           L0_ffn_shared_up_weight, L0_ffn_shared_down_weight):
    import numpy as np
    import concourse.bacc as bacc
    from concourse.bass_utils import run_bass_kernel_spmd

    x = np.ascontiguousarray(x)
    up, down = np.asarray(L0_ffn_up_weights), np.asarray(L0_ffn_down_weights)
    experts, inner, dim = up.shape
    up_t = np.concatenate([np.asarray(L0_ffn_shared_up_weight), up.reshape(experts * inner, dim)], axis=0).T
    down_t = np.concatenate([np.asarray(L0_ffn_shared_down_weight).T,
                             down.transpose(0, 2, 1).reshape(experts * inner, dim)], axis=0)
    columns = [np.asarray(v).reshape(-1, 128).T for v in (L0_xattn_ln_x_g, L0_xattn_ln_x_b,
                                                         L0_xattn_ln_l_g, L0_xattn_ln_l_b)]
    given = [x, ctx_1024, mask_BxS2_bk0, *columns, L0_xattn_q_gamma, L0_xattn_k_gamma, L0_xattn_W_q, L0_xattn_W_kv,
             L0_xattn_W_out, L0_xattn_b_out, np.asarray(L0_ffn_gate_weight).T, L0_ffn_gate_bias, up_t, down_t]

    nc = bacc.Bacc("TRN2", target_bir_lowering=False, num_devices=1)
    arrays, args = {}, []
    for name, a in zip(_INS, given):
        a = np.ascontiguousarray(a)
        arrays[f"in_{name}"] = a
        args.append(nc.dram_tensor(f"in_{name}", a.shape, mybir.dt.from_np(a.dtype), kind="ExternalInput").ap())
    out = nc.dram_tensor("out", x.shape, mybir.dt.float32, kind="ExternalOutput").ap()
    build(nc, *args, out)
    r = run_bass_kernel_spmd(nc, [arrays], core_ids=[0])
    return r.results[0]["out"]
```
